# Optimizing a Trainium2 kernel written in Bass

```python
import numpy as np
import jax
import jax.numpy as jnp

def _softmax(x, axis=-1):
    return jax.nn.softmax(x, axis=axis)

def _gelu(x):
    return jax.nn.gelu(x, approximate=True)

def _silu(x):
    return jax.nn.silu(x)

def _sigmoid(x):
    return jax.nn.sigmoid(x)

def _layernorm(x, axis=-1, eps=1e-05):
    m = jnp.mean(x, axis=axis, keepdims=True)
    v = jnp.var(x, axis=axis, keepdims=True)
    return (x - m) / jnp.sqrt(v + eps)

def _scatter_add(tgt, idx, src, axis=0):
    return tgt.at[idx].add(src)

def _segment_sum(src, seg, n):
    return jax.ops.segment_sum(src, seg, n)
kernel_name = 'mk_flamingo_gated_d1_seqx_r4_7aa1fc'

def setup_inputs(seed: int=0):
    np.random.seed(seed)
    _w = jnp.asarray

    def _rec_inputs():
        import jax
        import jax.numpy as jnp
        _rk = jax.random.key(seed)
        x = -0.0003929 + 0.9999 * jax.random.normal(jax.random.fold_in(_rk, 1), (4, 512, 1024), jnp.float32)
        _lenS = 512 - jax.random.randint(jax.random.fold_in(_rk, 7), (4,), 0, max(1, 512 // 4) + 1, jnp.int32)
        _lenS2 = 64 - jax.random.randint(jax.random.fold_in(_rk, 8), (4,), 0, max(1, 64 // 4) + 1, jnp.int32)
        _ctx_4096P = jax.random.normal(jax.random.fold_in(_rk, 11), (4, 16, 1024), jnp.float32)
        _ctx_4096c = jax.random.dirichlet(jax.random.fold_in(_rk, 511), 0.3 * jnp.ones((16,), jnp.float32), (4, 64))
        _ctx_4096t = jnp.einsum('bsk,bkd->bsd', _ctx_4096c, _ctx_4096P)
        _ctx_4096t = _ctx_4096t * jax.lax.rsqrt(jnp.mean(jnp.square(_ctx_4096t)) + 1e-12) * 0.953939
        ctx_4096 = 2.81802e-05 + 1.00001 * (_ctx_4096t + 0.3 * jax.random.normal(jax.random.fold_in(_rk, 611), (4, 64, 1024), jnp.float32))
        _g = jax.random.normal(jax.random.fold_in(_rk, 9001), (2, 1), jnp.float32)
        _g = jnp.sign(_g) * jnp.maximum(jnp.abs(_g), 1.0) + (_g == 0) * 1.0
        g_xattn = _g[0]
        g_ffn = _g[1]
        return (x, ctx_4096, g_xattn, g_ffn)
    x, ctx_4096, g_xattn, g_ffn = _rec_inputs()

    def _L0_xattn_setup():
        import jax, jax.numpy as jnp
        import numpy as np
        EMB_DIM = 1024
        NHEADS = 32
        KVHEADS = 8
        HEAD_DIM = 128
        ROPE_BASE = 10000.0

        def _rope(x):
            B, H, S, D = x.shape
            inv_freq = 1.0 / ROPE_BASE ** (jnp.arange(0, D, 2, dtype=jnp.float32) / D)
            ang = jnp.arange(S, dtype=jnp.float32)[:, None] * inv_freq[None, :]
            cos = jnp.concatenate([jnp.cos(ang), jnp.cos(ang)], axis=-1)
            sin = jnp.concatenate([jnp.sin(ang), jnp.sin(ang)], axis=-1)
            x1, x2 = (x[..., :D // 2], x[..., D // 2:])
            rot = jnp.concatenate([-x2, x1], axis=-1)
            return x * cos + rot * sin
        key = jax.random.key(seed)
        ks = jax.random.split(key, 7)
        B, S = (2, 512)
        std_qk = EMB_DIM ** (-0.5)
        std_vd = (1.0 / (EMB_DIM * NHEADS * HEAD_DIM) ** 0.5) ** 0.5
        return {'q': jax.random.normal(ks[0], (B, S, EMB_DIM), jnp.float32), 'k': jax.random.normal(ks[1], (B, S, EMB_DIM), jnp.float32), 'v': jax.random.normal(ks[2], (B, S, EMB_DIM), jnp.float32), 'Wq': jax.random.normal(ks[3], (NHEADS * HEAD_DIM, EMB_DIM), jnp.float32) * std_qk, 'Wk': jax.random.normal(ks[4], (KVHEADS * HEAD_DIM, EMB_DIM), jnp.float32) * std_qk, 'Wv': jax.random.normal(ks[5], (KVHEADS * HEAD_DIM, EMB_DIM), jnp.float32) * std_vd, 'Wd': jax.random.normal(ks[6], (EMB_DIM, NHEADS * HEAD_DIM), jnp.float32) * std_vd}
    _L0_xattn_all = _L0_xattn_setup()
    _L0_xattn_in = {k: v for k, v in _L0_xattn_all.items() if k in ('Wq', 'Wk', 'Wv', 'Wd')}
    del _L0_xattn_all

    def _L0_ffn_setup():
        import jax, jax.numpy as jnp
        import numpy as np
        NUM_EXPERTS = 16
        TOP_K = 2
        INTER = 112
        key = jax.random.key(seed)
        k1, k2, k3, k4, k5 = jax.random.split(key, 5)
        B, S, H = (4, 512, 1024)
        scale = 0.02
        return {'hid': jax.random.normal(k1, (B, S, H), dtype=jnp.float32), 'gate_w': jax.random.normal(k2, (NUM_EXPERTS, H), dtype=jnp.float32) * scale, 'u': jax.random.normal(k3, (NUM_EXPERTS * INTER, H), dtype=jnp.float32) * scale, 'g': jax.random.normal(k4, (NUM_EXPERTS * INTER, H), dtype=jnp.float32) * scale, 'd': jax.random.normal(k5, (H, NUM_EXPERTS * INTER), dtype=jnp.float32) * scale}
    _L0_ffn_all = _L0_ffn_setup()
    _L0_ffn_in = {k: v for k, v in _L0_ffn_all.items() if k in ('gate_w', 'u', 'g', 'd')}
    del _L0_ffn_all
    return {'x': x, 'ctx_4096': ctx_4096, 'g_xattn': g_xattn, 'g_ffn': g_ffn, 'L0_xattn_Wq': _L0_xattn_in['Wq'], 'L0_xattn_Wk': _L0_xattn_in['Wk'], 'L0_xattn_Wv': _L0_xattn_in['Wv'], 'L0_xattn_Wd': _L0_xattn_in['Wd'], 'L0_ffn_gate_w': _L0_ffn_in['gate_w'], 'L0_ffn_u': _L0_ffn_in['u'], 'L0_ffn_g': _L0_ffn_in['g'], 'L0_ffn_d': _L0_ffn_in['d']}

def reference(x, ctx_4096, g_xattn, g_ffn, L0_xattn_Wq, L0_xattn_Wk, L0_xattn_Wv, L0_xattn_Wd, L0_ffn_gate_w, L0_ffn_u, L0_ffn_g, L0_ffn_d):
    import jax
    import jax.numpy as jnp

    def _L0_xattn_ref(q, k, v, Wq, Wk, Wv, Wd):
        import jax, jax.numpy as jnp
        import numpy as np
        EMB_DIM = 1024
        NHEADS = 32
        KVHEADS = 8
        HEAD_DIM = 128
        ROPE_BASE = 10000.0

        def _rope(x):
            B, H, S, D = x.shape
            inv_freq = 1.0 / ROPE_BASE ** (jnp.arange(0, D, 2, dtype=jnp.float32) / D)
            ang = jnp.arange(S, dtype=jnp.float32)[:, None] * inv_freq[None, :]
            cos = jnp.concatenate([jnp.cos(ang), jnp.cos(ang)], axis=-1)
            sin = jnp.concatenate([jnp.sin(ang), jnp.sin(ang)], axis=-1)
            x1, x2 = (x[..., :D // 2], x[..., D // 2:])
            rot = jnp.concatenate([-x2, x1], axis=-1)
            return x * cos + rot * sin
        B, Sq, _ = q.shape
        Skv = k.shape[1]
        queries = (q @ Wq.T).reshape(B, Sq, NHEADS, HEAD_DIM).transpose(0, 2, 1, 3)
        keys = (k @ Wk.T).reshape(B, Skv, KVHEADS, HEAD_DIM).transpose(0, 2, 1, 3)
        values = (v @ Wv.T).reshape(B, Skv, KVHEADS, HEAD_DIM).transpose(0, 2, 1, 3)
        queries = _rope(queries)
        keys = _rope(keys)
        exp = NHEADS // KVHEADS
        keys = jnp.repeat(keys, exp, axis=1)
        values = jnp.repeat(values, exp, axis=1)
        scale = HEAD_DIM ** (-0.5)
        scores = jnp.einsum('bhqd,bhkd->bhqk', queries, keys) * scale
        causal = jnp.tril(jnp.ones((Sq, Skv), dtype=bool))
        scores = jnp.where(causal[None, None], scores, jnp.finfo(scores.dtype).min)
        attn = jax.nn.softmax(scores, axis=-1)
        ctx = jnp.einsum('bhqk,bhkd->bhqd', attn, values)
        ctx = ctx.transpose(0, 2, 1, 3).reshape(B, Sq, NHEADS * HEAD_DIM)
        return ctx @ Wd.T

    def _L0_ffn_ref(hid, gate_w, u, g, d):
        import jax, jax.numpy as jnp
        import numpy as np
        NUM_EXPERTS = 16
        TOP_K = 2
        INTER = 112
        B, S, H = hid.shape
        x = hid.reshape(-1, H)
        bs = x.shape[0]
        logits = x @ gate_w.T
        probs = jax.nn.softmax(logits.astype(jnp.float32), axis=-1)
        vals, idx = jax.lax.top_k(probs, TOP_K)
        vals = vals / jnp.sum(vals, axis=-1, keepdims=True)
        rows = jnp.arange(bs)[:, None]
        w = jnp.zeros((bs, NUM_EXPERTS), dtype=jnp.float32).at[rows, idx].set(vals)
        w = w.astype(x.dtype)
        gate_out = (x @ g.T).reshape(bs, NUM_EXPERTS, INTER)
        up_out = (x @ u.T).reshape(bs, NUM_EXPERTS, INTER)
        h = jax.nn.silu(gate_out) * up_out
        d_r = d.reshape(H, NUM_EXPERTS, INTER)
        out = jnp.einsum('bei,hei,be->bh', h, d_r, w)
        return out.reshape(B, S, H)
    x = x + jnp.tanh(g_xattn[0]) * _L0_xattn_ref(_layernorm(x, axis=-1), ctx_4096, ctx_4096, L0_xattn_Wq, L0_xattn_Wk, L0_xattn_Wv, L0_xattn_Wd)
    x = x + jnp.tanh(g_ffn[0]) * _L0_ffn_ref(_layernorm(x, axis=-1), L0_ffn_gate_w, L0_ffn_u, L0_ffn_g, L0_ffn_d)
    return x

_drawn_inputs = setup_inputs


def setup_inputs(seed=0):
    import zlib

    import numpy as np

    out = dict(_drawn_inputs(seed))
    spreads = {}
    factors = {}
    for name, (base, spread) in spreads.items():
        noise = np.random.default_rng([zlib.crc32(name.encode()), seed]).standard_normal(out[name].shape)
        drawn = base * np.exp(spread * noise) if base else spread * noise
        out[name] = jnp.asarray(drawn.astype(out[name].dtype))
    for name, factor in factors.items():
        out[name] = (out[name] * factor).astype(out[name].dtype)
    return out
```

```python
import numpy as np
import concourse.bass as bass
from concourse import mybir
from contextlib import ExitStack

B, S, C = 4, 512, 1024
SK = 64
NH, NKV, D = 32, 8, 128
NE, FI = 16, 112
P = 128
T = B * S
KC = C // P
BP = B // 2
HG = NH // NKV
NG = BP * NKV
QT = S // P
TP = 2 * QT
HALF = C // 2
CAP = T
ET = CAP // P
MT = 2 * T // P + NE
SCALE = float(D) ** -0.5
EPS = 1e-5
MASKED = -2.0 ** 127
GW = 256
E_CHAIN = 9
CHAIN = 14


def program(nc, x, ctx_t, g_x, g_f, wq, wk, wv, wd, gate, gu, dn, cos, sin, mask, ident, tri, out):
    f32, f32r, i32, u32 = mybir.dt.float32, mybir.dt.float32r, mybir.dt.int32, mybir.dt.uint32
    ALU, ACT, X = mybir.AluOpType, mybir.ActivationFunctionType, mybir.AxisListType.X

    keep = ExitStack()
    with keep:
        def sem(name):
            return keep.enter_context(nc.semaphore(name))

        def sb(stack, name, shape, dt=f32):
            return stack.enter_context(nc.sbuf_tensor(name, shape, dt))

        ds, ts = bass.ds, bass.ts

        def wait(eng, s, value):
            if not isinstance(value, int) or value > 0:
                eng.wait_ge(s, value)

        k_hbm = nc.dram_tensor("k_hbm", (NKV, D, B * SK), f32).ap()
        v_hbm = nc.dram_tensor("v_hbm", (NKV, D, B * SK), f32).ap()
        xn_hbm = nc.dram_tensor("xn_hbm", (T + P, C), f32).ap()
        slots_hbm = nc.dram_tensor("slots_hbm", (NE * CAP, 2), f32).ap()

        idn = sb(keep, "idn", [P, P])
        tri_sb = sb(keep, "tri_sb", [P, P])
        ones = sb(keep, "ones", [P, P])
        eps_half = sb(keep, "eps_half", [P, 1])
        tanh_x = sb(keep, "tanh_x", [P, 1])
        tanh_f = sb(keep, "tanh_f", [P, 1])
        gates_raw = sb(keep, "gates_raw", [P, 2])
        count = sb(keep, "count", [P, NE])
        tile_n = sb(keep, "tile_n", [P, NE], i32)
        tile_at = sb(keep, "tile_at", [P, NE + 1], i32)

        bank = [keep.enter_context(nc.psum_tensor(f"bank{i}", [P, 512], f32)) for i in range(8)]
        q_ps = bank[0:2]
        st_ps = bank[2]
        sn_ps = bank[3]
        pt_ps = bank[4]
        ov_ps = bank[5:8]

        att = ExitStack()
        xh = sb(att, "xh", [P, KC, 2 * S], f32r)
        xl = sb(att, "xl", [P, KC, 2 * S], f32r)
        acc = sb(att, "acc", [P, TP, C])
        kcur = sb(att, "kcur", [P, 2 * SK])
        vraw = sb(att, "vraw", [P, 3 * SK])
        vh = sb(att, "vh", [P, 3 * SK], f32r)
        vl = sb(att, "vl", [P, 3 * SK], f32r)
        wq_raw = sb(att, "wq_raw", [P, 2, HALF])
        wqh = sb(att, "wqh", [P, 4, HALF], f32r)
        wql = sb(att, "wql", [P, 4, HALF], f32r)
        wd_raw = sb(att, "wd_raw", [P, 2, HALF])
        wdh = sb(att, "wdh", [P, 2, HALF], f32r)
        wdl = sb(att, "wdl", [P, 2, HALF], f32r)
        cos_sb = sb(att, "cos_sb", [P, S])
        sin_sb = sb(att, "sin_sb", [P, S])
        mask_sb = sb(att, "mask_sb", [P, SK])
        qr = sb(att, "qr", [P, 4, S])
        qt2 = sb(att, "qt2", [P, 2, S])
        soft = sb(att, "soft", [P, 3, S])
        mx = sb(att, "mx", [P, 2, 8])
        sm = sb(att, "sm", [P, 2, 8])
        rc = sb(att, "rc", [P, 2, 8])
        stats = sb(att, "stats", [P, 2, 2, 6])
        mv = sb(att, "mv", [P, 2, 2])
        var_eps = sb(att, "var_eps", [P, 2, 1])
        rstd = sb(att, "rstd", [P, 2, 1])
        gate_sb = sb(att, "gate_sb", [P, KC, NE])
        xt2 = soft[:, 0:2, :].rearrange("p a q -> p (a q)").rearrange("p (k t) -> p k t", k=KC)
        lgt = sb(att, "lgt", [NE, P])
        lg = sb(att, "lg", [P, NE])
        top = sb(att, "top", [P, 8])
        top_i = sb(att, "top_i", [P, 8], u32)
        top_f = sb(att, "top_f", [P, 2])
        iota_e = sb(att, "iota_e", [P, NE])
        iota_p = sb(att, "iota_p", [P, 1])
        hot = sb(att, "hot", [P, 3, NE])
        pos = sb(att, "pos", [P, NE])
        pick = sb(att, "pick", [P, 2, NE])
        pos_k = sb(att, "pos_k", [P, 2])
        slot_f = sb(att, "slot_f", [P, 2])
        slot_i = sb(att, "slot_i", [P, 2], i32)
        gap = sb(att, "gap", [P, 1])
        egap = sb(att, "egap", [P, 1])
        den = sb(att, "den", [P, 1])
        w1 = sb(att, "w1", [P, 1])
        pair = sb(att, "pair", [P, 2, 2])
        empty = sb(att, "empty", [P, P, 2])

        early = ExitStack()
        ctx_sb = sb(early, "ctx_sb", [P, KC, B * SK])
        wkv = sb(early, "wkv", [P, 4, KC * D])
        k1 = sb(early, "k1", [P, 2, B * SK])
        k2 = sb(early, "k2", [P, 2, B * SK])
        v1 = sb(early, "v1", [P, 2, B * SK])
        early.close()
        pth = sb(att, "pth", [P, 2, 2, S], f32r)
        ptl = sb(att, "ptl", [P, 2, 2, S], f32r)
        vwh = sb(att, "vwh", [P, 2, 2, C], f32r)
        vwl = sb(att, "vwl", [P, 2, 2, C], f32r)
        att.close()

        ffn = ExitStack()
        gu_raw = sb(ffn, "gu_raw", [P, 2, KC * 2 * FI])
        guh = sb(ffn, "guh", [P, 2, KC, GW], f32r)
        gul = sb(ffn, "gul", [P, 2, KC, GW], f32r)
        dn_raw = sb(ffn, "dn_raw", [FI, 2, C])
        dnh = sb(ffn, "dnh", [FI, 2, C], f32r)
        over_acc = sb(ffn, "over_acc", [P, C // 2])
        dnl = sb(ffn, "dnl", [FI, 2, C], f32r)
        xg = sb(ffn, "xg", [P, C])
        xfh = sb(ffn, "xfh", [P, KC, P], f32r)
        xfl = sb(ffn, "xfl", [P, KC, P], f32r)
        sg = sb(ffn, "sg", [P, FI])
        hm = sb(ffn, "hm", [P, FI])
        hth = sb(ffn, "hth", [FI, P], f32r)
        htl = sb(ffn, "htl", [FI, P], f32r)
        ys = sb(ffn, "ys", [P, C])
        lists = sb(ffn, "lists", [P, 2, 2 * P])
        row_all = sb(ffn, "row_all", [P, NE * ET], i32)
        w_all = sb(ffn, "w_all", [P, NE * ET])
        row_of = sb(ffn, "row_of", [P, MT + ET], i32)
        w_of = sb(ffn, "w_of", [P, MT + ET])
        row_g = sb(ffn, "row_g", [P, 1], i32)
        row_s = sb(ffn, "row_s", [P, 1], i32)
        pre = sb(ffn, "pre", [P, 2, NE])
        ffn.close()

        s_const = sem("s_const")
        s_ctx = sem("s_ctx")
        s_kw = [sem(f"s_kw{i}") for i in range(4)]
        s_kvout = [sem(f"s_kvout{i}") for i in range(4)]
        s_x = [sem(f"s_x{i}") for i in range(TP)]
        s_wq = [sem(f"s_wq{i}") for i in range(2)]
        s_wd = [sem(f"s_wd{i}") for i in range(2)]
        s_k = sem("s_k")
        s_v = sem("s_v")
        s_x1 = [sem(f"s_x1_{i}") for i in range(TP)]
        s_xn = [sem(f"s_xn{i}") for i in range(2)]
        s_zero = sem("s_zero")
        s_slot0 = sem("s_slot0")
        s_scat = [sem(f"s_scat{i}") for i in range(2)]
        setup = sem("setup")
        tanh_done = sem("tanh_done")
        iotas = sem("iotas")
        kproj, vproj = sem("kproj"), sem("vproj")
        krot, kst, vst = sem("krot"), sem("kst"), sem("vst")
        stat_done, aggr_done, var_done, rstd_done, xn_done = (sem(n) for n in ("stat_done", "aggr_done", "var_done", "rstd_done", "xn_done"))
        xt_done, xt_hi, xt_lo = sem("xt_done"), sem("xt_hi"), sem("xt_lo")
        wq_hi, wq_lo, wd_hi, wd_lo = (sem(n) for n in ("wq_hi", "wq_lo", "wd_hi", "wd_lo"))
        v_hi, v_lo = sem("v_hi"), sem("v_lo")
        q_done, q_rot, q_ready = sem("q_done"), sem("q_rot"), sem("q_ready")
        s_done, st_mask, st_copy = sem("s_done"), sem("st_mask"), sem("st_copy")
        t1_done, mx_done, sub_done, exp_done = (sem(n) for n in ("t1_done", "mx_done", "sub_done", "exp_done"))
        sum_done, rc_done, p_done = sem("sum_done"), sem("rc_done"), sem("p_done")
        t2_done, pt_hi, pt_lo = sem("t2_done"), sem("pt_hi"), sem("pt_lo")
        ov_done, vw_hi, ov_free = sem("ov_done"), sem("vw_hi"), sem("ov_free")
        xt2_done = sem("xt2_done")
        lg_done, lgt_done, lgn_done = sem("lg_done"), sem("lgt_done"), sem("lgn_done")
        r_chain, gap_done, egap_done = sem("r_chain"), sem("gap_done"), sem("egap_done")
        hot_done, cnt_mm = sem("hot_done"), sem("cnt_mm")

        s_gu = [sem(f"s_gu{i}") for i in range(2)]
        s_dn = [sem(f"s_dn{i}") for i in range(2)]
        s_lists, s_gather, s_add = sem("s_lists"), sem("s_gather"), sem("s_add")
        lists_done, rows_done = sem("lists_done"), sem("rows_done")
        e_chain = sem("e_chain")
        w_hi, w_lo, pads = sem("w_hi"), sem("w_lo"), sem("pads")
        rows_chain, w_chain = sem("rows_chain"), sem("w_chain")
        tt_done, xf_hi, xf_lo, gu_done = sem("tt_done"), sem("xf_hi"), sem("xf_lo"), sem("gu_done")
        silu_done, h_done, ht_done, ht_hi, ht_lo = (sem(n) for n in ("silu_done", "h_done", "ht_done", "ht_hi", "ht_lo"))
        d_done, y_a, y_b = sem("d_done"), sem("y_a"), sem("y_b")
        xf_ps, gu_ps, ht_ps, y_ps = bank[0:2], bank[2], bank[3], bank[4:6]


        block = keep.enter_context(nc.Block())


        def in_units(n, prev, cur, unit):
            for u in range(2 * HG):
                unit(n, u, prev, cur)

        def turns(eng, bp, turn, last_apart=False):
            turn(bp * NKV, 0, False, True)
            end = NKV - 1 if last_apart else NKV
            with eng.Fori(1, end) as g:
                turn(g + bp * NKV, g, True, True)
            if last_apart:
                turn(bp * NKV + NKV - 1, NKV - 1, True, True)
            turn(bp * NKV + NKV, NKV, True, False)


        def scatter_slots(pool, i):
            pool.wait_ge(r_chain, (i + 1) * CHAIN)
            if i == 0:
                pool.wait_ge(s_slot0, 16 * (NE * ET // P))
            for k in range(2):
                pool.indirect_dma_start(out=slots_hbm, out_offset=bass.IndirectOffsetOnAxis(ap=slot_i[:, k:k + 1], axis=0),
                                        in_=pair[:, k, :], in_offset=None).then_inc(s_scat[k], 16)


        def experts(eng, tile, first, tail):
            def expert(e, r, is_first, is_last):
                t0 = 0 if is_first else eng.value_load(tile_at[0:1, ds(e, 1)], min_val=1, max_val=MT)
                t1 = eng.value_load(tile_at[0:1, ds(e + 1, 1)], min_val=1, max_val=MT)
                first(e, r, t0, is_last)
                with eng.If(t1 > t0 + 1):
                    with eng.Fori(t0 + 1, t1) as t:
                        tile(t, r)

            expert(0, 0, True, False)
            expert(1, 1, False, False)
            with eng.Fori(1, NE // 2 - 1) as ep:
                for r in range(2):
                    expert(ep * 2 + r, r, False, False)
            expert(NE - 2, 0, False, False)
            expert(NE - 1, 1, False, True)
            tail(eng.value_load(tile_at[0:1, NE:NE + 1], min_val=NE, max_val=MT))

        @block.sync
        def _(sp):
            sp.dma_start(ctx_sb[:], ctx_t).then_inc(s_ctx, 16)
            sp.dma_start(gates_raw[:, 0:1], g_x.partition_broadcast(P)).then_inc(s_const, 16)
            sp.dma_start(gates_raw[:, 1:2], g_f.partition_broadcast(P)).then_inc(s_const, 16)
            sp.dma_start(cos_sb[:], cos).then_inc(s_const, 16)
            sp.dma_start(sin_sb[:], sin).then_inc(s_const, 16)

            def kv_weights(g, r):
                sp.dma_start(wkv[:, r, :], wk[g]).then_inc(s_kw[r], 16)
                sp.dma_start(wkv[:, 2 + r, :], wv[g]).then_inc(s_kw[2 + r], 16)

            def kv_store(g, r):
                sp.wait_ge(kst, g + 1)
                sp.dma_start(k_hbm[g], k1[:, r, :]).then_inc(s_kvout[r], 16)
                sp.wait_ge(vst, g + 1)
                sp.dma_start(v_hbm[g], v1[:, r, :]).then_inc(s_kvout[2 + r], 16)

            for r in range(2):
                kv_weights(r, r)
            sp.dma_start(mask_sb[:], mask).then_inc(s_const, 16)
            sp.dma_start(idn[:], ident).then_inc(s_const, 16)
            sp.dma_start(tri_sb[:], tri).then_inc(s_const, 16)
            sp.dma_start(gate_sb[:], gate).then_inc(s_const, 16)
            with sp.Fori(1, NKV // 2) as i:
                for r in range(2):
                    sp.wait_ge(vproj, i * 2 - 1 + r)
                    kv_weights(i * 2 + r, r)
                    kv_store(i * 2 - 2 + r, r)
            for r in range(2):
                kv_store(NKV - 2 + r, r)

            def load_wq(n, head, u):
                wait(sp, wq_lo, n * 8 + u - 1)
                sp.dma_start(wq_raw[:, u % 2, :], wq[head, :, (u % 2) * HALF:(u % 2 + 1) * HALF]).then_inc(s_wq[u % 2], 16)

            def load_wd(n, head, u):
                wait(sp, wd_lo, n * 8 + u - 1)
                sp.dma_start(wd_raw[:, u % 2, :], wd[head, :, (u % 2) * HALF:(u % 2 + 1) * HALF]).then_inc(s_wd[u % 2], 16)

            for u in range(2):
                load_wq(0, 0, u)

            for bp in range(BP):
                for t in range(TP):
                    if bp:
                        sp.wait_ge(s_x1[t], 16)
                    row = (bp * TP + t) * P
                    sp.dma_start(acc[:, t, :], x[row:row + P, :]).then_inc(s_x[t], 16)
                if bp == 0:
                    for r in range(4):
                        sp.wait_ge(s_kvout[r], 16 * (NKV // 2))

                def turn(n, g, prev, cur):
                    last = isinstance(n, int) and n == NG - 1
                    for u in range(2 * HG):
                        if cur and u < 6:
                            load_wq(n, g * HG + (u + 2) // 2, u + 2)
                        elif cur and not last:
                            nxt = 0 if isinstance(g, int) and g == NKV - 1 else g * HG + HG
                            load_wq(n + 1, nxt, u - 6)
                        if u == 0 and prev:
                            for d in (6, 7):
                                load_wd(n - 1, g * HG - 1, d)
                        if not cur:
                            continue
                        if u == 1:
                            wait(sp, s_done, n * 4)
                            sp.dma_start(kcur[:], k_hbm[g, :, bp * 2 * SK:(bp + 1) * 2 * SK]).then_inc(s_k, 16)
                            wait(sp, v_lo, n)
                            sp.dma_start(vraw[:, 0:2 * SK], v_hbm[g, :, bp * 2 * SK:(bp + 1) * 2 * SK]).then_inc(s_v, 16)
                            sp.dma_start(vraw[:, 2 * SK:3 * SK], v_hbm[g, :, bp * 2 * SK:bp * 2 * SK + SK]).then_inc(s_v, 16)
                        for d in {3: (0,), 4: (1,), 6: (2, 3), 7: (4, 5)}.get(u, ()):
                            load_wd(n, g * HG + d // 2, d)

                turns(sp, bp, turn, last_apart=True)

                sp.wait_ge(ov_free, 24 * NKV * (bp + 1))
                for t in range(TP):
                    row = (bp * TP + t) * P
                    sp.dma_start(out[row:row + P, :], acc[:, t, :]).then_inc(s_x1[t], 16)
                for t in range(TP):
                    row = (bp * TP + t) * P
                    sp.wait_ge(xn_done, 2 * TP * bp + TP + t + 1)
                    r = t % 2
                    sp.dma_start(xn_hbm[row:row + P, :], qr[:, 2 * r:2 * r + 2, :].rearrange("p a q -> p (a q)")).then_inc(s_xn[r], 16)

            for k in range(2):
                sp.wait_ge(s_scat[k], 16 * TP * BP)
            for t in range(TP):
                sp.wait_ge(s_x1[t], 16 * BP)
            for r in range(2):
                sp.wait_ge(s_xn[r], 16 * (TP // 2) * BP)
            sp.dma_start(lists[:], slots_hbm.rearrange("(h a s) c -> a h (s c)", h=2, s=P)).then_inc(s_lists, 16)

            def expert_weights(e, r):
                sp.dma_start(gu_raw[:, r, :], gu[e]).then_inc(s_gu[r], 16)
                sp.dma_start(dn_raw[:, r, :], dn[e]).then_inc(s_dn[r], 16)

            for r in range(2):
                expert_weights(r, r)
            with sp.Fori(1, NE // 2) as ep:
                for r in range(2):
                    sp.wait_ge(w_lo, ep * 2 - 1 + r)
                    expert_weights(ep * 2 + r, r)

        @block.tensor
        def _(pe):
            pe.wait_ge(s_ctx, 16)

            def kv_project(i, r):
                pe.wait_ge(s_kw[r], i * 16 + 16)
                wait(pe, krot, i * 2 + r - 1)
                for k in range(KC):
                    mm = pe.matmul(bank[r][:, 0:B * SK], wkv[:, r, k * D:(k + 1) * D], ctx_sb[:, k, :], start=(k == 0), stop=(k == KC - 1))
                mm.then_inc(kproj, 1)
                pe.wait_ge(s_kw[2 + r], i * 16 + 16)
                wait(pe, vst, i * 2 + r - 1)
                for k in range(KC):
                    mm = pe.matmul(bank[2 + r][:, 0:B * SK], wkv[:, 2 + r, k * D:(k + 1) * D], ctx_sb[:, k, :], start=(k == 0), stop=(k == KC - 1))
                mm.then_inc(vproj, 1)

            for r in range(2):
                kv_project(0, r)
            with pe.Fori(1, NKV // 2) as i:
                for r in range(2):
                    kv_project(i, r)
            pe.wait_ge(s_const, 16 * 8)

            def turn_tile(m, r):
                pe.wait_ge(xn_done, m + 1)
                for k in range(KC):
                    mm = pe.transpose(bank[2 * r + k // 4][:, ts(k % 4, P)], qr[:, 2 * r + k // 4, ts(k % 4, P)], idn[:])
                mm.then_inc(xt_done, 1)

            def norm_x(bp, i, r):
                wait(pe, xt_lo, i * 2 + r - 1)
                turn_tile(i * 2 + r + bp * TP, r)

            def q_unit(n, u):
                j, b = u // 2, u % 2
                wait(pe, q_rot, n * 8 + u - 1)
                for kh in range(2):
                    if b == 0:
                        pe.wait_ge(wq_lo, n * 8 + 2 * j + kh + 1)
                    slot = (2 * j + kh) % 4
                    for kk in range(4):
                        k = 4 * kh + kk
                        cols = slice(b * S, (b + 1) * S)
                        pe.matmul(q_ps[b][:], wqh[:, slot, ts(kk, D)], xh[:, k, cols], start=(k == 0), stop=False)
                        pe.matmul(q_ps[b][:], wqh[:, slot, ts(kk, D)], xl[:, k, cols], start=False, stop=False)
                        mm = pe.matmul(q_ps[b][:], wql[:, slot, ts(kk, D)], xh[:, k, cols], start=False, stop=(k == KC - 1))
                mm.then_inc(q_done, 1)

            def scores(m, c, b):
                s = 4 * m + 2 * c + b if isinstance(m, int) else m * 4 + (2 * c + b)
                pe.wait_ge(q_ready, m * 8 + 4 * c + 2 + b + 1)
                pe.wait_ge(s_k, m * 16 + 16)
                wait(pe, st_copy, s)
                wait(pe, st_mask, s)
                for hh in range(2):
                    at = SK * (hh ^ b)
                    mm = pe.matmul(st_ps[at:at + SK, :], kcur[:, ts(b, SK)], qr[:, 2 * hh + b, :], start=True, stop=True)
                mm.then_inc(s_done, 1)

            def turn_scores(m, c, b):
                s = m * 4 + (2 * c + b)
                pe.wait_ge(st_copy, s + 1)
                pe.wait_ge(st_mask, s + 1)
                wait(pe, sub_done, s)
                for q in range(QT):
                    mm = pe.transpose(sn_ps[:, ts(q, P)], soft[:, 0, ts(q, P)], idn[:])
                mm.then_inc(t1_done, 1)

            def turn_probs(m, c, b):
                s = m * 4 + (2 * c + b)
                pe.wait_ge(p_done, s + 1)
                wait(pe, pt_lo, s)
                for q in range(QT):
                    mm = pe.transpose(pt_ps[:, ts(q, P)], soft[:, 1 + b, ts(q, P)], idn[:])
                mm.then_inc(t2_done, 1)

            def values_out(m, j):
                pe.wait_ge(v_lo, m + 1)
                cols = slice(0, 2 * SK) if j % 2 == 0 else slice(SK, 3 * SK)
                for half in range(2):
                    pe.wait_ge(wd_lo, m * 8 + 2 * j + half + 1)
                    wait(pe, ov_free, m * 24 + 2 * j + half - 2)
                    ps = ov_ps[(2 * j + half) % 3]
                    pe.matmul(ps[:], vh[:, cols], wdh[:, half, :], start=True, stop=False)
                    pe.matmul(ps[:], vh[:, cols], wdl[:, half, :], start=False, stop=False)
                    pe.matmul(ps[:], vl[:, cols], wdh[:, half, :], start=False, stop=True).then_inc(ov_done, 1)

            def outputs(m):
                pe.wait_ge(pt_lo, m * 4 + 4)
                for o in range(16):
                    b, q, half = o // 8, o // 2 % 4, o % 2
                    pe.wait_ge(ov_free, m * 24 + max(8, 8 + o - 2))
                    ps = ov_ps[(8 + o) % 3]
                    for c in range(2):
                        ph, pl = pth[:, c, b, ts(q, P)], ptl[:, c, b, ts(q, P)]
                        wh, wl = vwh[:, c, b, ts(half, HALF)], vwl[:, c, b, ts(half, HALF)]
                        pe.matmul(ps[:], ph, wh, start=(c == 0), stop=False)
                        pe.matmul(ps[:], ph, wl, start=False, stop=False)
                        mm = pe.matmul(ps[:], pl, wh, start=False, stop=(c == 1))
                    mm.then_inc(ov_done, 1)

            def turn(n, g, prev, cur):
                m = n - 1
                for u in range(2 * HG):
                    if cur:
                        q_unit(n, u)
                    if prev and u == 0:
                        turn_scores(m, 1, 0)
                        scores(m, 1, 1)
                        values_out(m, 3)
                    if prev and u == 1:
                        turn_scores(m, 1, 1)
                    if prev and u == 2:
                        turn_probs(m, 1, 0)
                    if prev and u == 3:
                        turn_probs(m, 1, 1)
                    if cur and u == 3:
                        scores(n, 0, 0)
                    if prev and u == 4:
                        outputs(m)
                    if not cur:
                        continue
                    if u == 4:
                        turn_scores(n, 0, 0)
                        scores(n, 0, 1)
                    if u == 5:
                        values_out(n, 0)
                        turn_scores(n, 0, 1)
                    if u == 6:
                        turn_probs(n, 0, 0)
                        values_out(n, 1)
                    if u == 7:
                        turn_probs(n, 0, 1)
                        values_out(n, 2)
                        scores(n, 1, 0)

            def route(bp, t):
                i = bp * TP + t
                pe.wait_ge(xt2_done, i + 1)
                for k in range(KC):
                    mm = pe.matmul(bank[4][0:NE, 0:P], gate_sb[:, k, :], xt2[:, k, :], start=(k == 0), stop=(k == KC - 1))
                mm.then_inc(lg_done, 1)
                pe.wait_ge(lgt_done, i + 1)
                pe.transpose(bank[5][:, 0:NE], lgt[:], idn[0:NE, 0:NE]).then_inc(lgn_done, 1)
                pe.wait_ge(hot_done, i + 1)
                pe.matmul(bank[6][:, 0:NE], tri_sb[:], hot[:, 2, :], start=True, stop=True)
                pe.matmul(bank[6][:, NE:2 * NE], ones[:], hot[:, 2, :], start=True, stop=True).then_inc(cnt_mm, 1)

            for bp in range(BP):
                if bp:
                    pe.wait_ge(xt2_done, TP)
                for t in range(TP):
                    norm_x(bp, bp * QT + t // 2, t % 2)
                pe.wait_ge(xt_lo, (bp + 1) * TP)
                turns(pe, bp, turn)
                for t in range(TP):
                    if t >= 2:
                        pe.wait_ge(xt2_done, bp * TP + t - 1)
                    turn_tile(2 * TP * bp + TP + t, t % 2)
                    if t:
                        route(bp, t - 1)
                route(bp, TP - 1)

            pe.wait_ge(s_lists, 16)
            pe.wait_ge(e_chain, 1)
            for h in range(2):
                for c in range(2):
                    mm = pe.transpose(bank[4 + c][:, ts(h, P)], lists[:, h, c:2 * P:2], idn[:])
            mm.then_inc(lists_done, 1)
            pe.wait_ge(e_chain, E_CHAIN)

            def turn_rows(t):
                pe.wait_ge(s_gather, t * 16 + 16)
                wait(pe, xf_lo, t)
                for k in range(KC):
                    mm = pe.transpose(xf_ps[k // 4][:, ts(k % 4, P)], xg[:, ts(k, P)], idn[:])
                mm.then_inc(tt_done, 1)

            def finish(t, r):
                pe.wait_ge(h_done, t)
                pe.transpose(ht_ps[0:FI, 0:P], hm[:], idn[:]).then_inc(ht_done, 1)
                pe.wait_ge(ht_lo, t)
                for half in range(2):
                    cols = ts(half, HALF)
                    pe.matmul(y_ps[half][:], hth[:], dnh[:, r, cols], start=True, stop=False)
                    pe.matmul(y_ps[half][:], hth[:], dnl[:, r, cols], start=False, stop=False)
                    mm = pe.matmul(y_ps[half][:], htl[:], dnh[:, r, cols], start=False, stop=True)
                mm.then_inc(d_done, 1)

            def gate_up(t, r):
                pe.wait_ge(xf_lo, t + 1)
                for k in range(KC):
                    pe.matmul(gu_ps[:, 0:GW], xfh[:, k, :], guh[:, r, k, :], start=(k == 0), stop=False)
                    pe.matmul(gu_ps[:, 0:GW], xfh[:, k, :], gul[:, r, k, :], start=False, stop=False)
                    mm = pe.matmul(gu_ps[:, 0:GW], xfl[:, k, :], guh[:, r, k, :], start=False, stop=(k == KC - 1))
                mm.then_inc(gu_done, 1)

            def tile(t, r):
                turn_rows(t)
                finish(t, r)
                gate_up(t, r)

            def first(e, r, t, is_last):
                turn_rows(t)
                if not (isinstance(e, int) and e == 0):
                    finish(t, 1 - r)
                pe.wait_ge(w_lo, e + 1)
                gate_up(t, r)

            experts(pe, tile, first, lambda t: finish(t, (NE - 1) % 2))

        @block.vector
        def _(dve):
            dve.memset(ones[:], 1.0).then_inc(setup, 1)
            dve.memset(count[:], 0.0).then_inc(setup, 1)
            dve.wait_ge(s_const, 16 * 8)

            def kv_rotate(i, r):
                g = i * 2 + r
                dve.wait_ge(kproj, g + 1)
                wait(dve, s_kvout[r], i * 16)
                rows = slice(0, D // 2), slice(D // 2, D)
                kin = bank[r][:, 0:B * SK].rearrange("p (b s) -> p b s", b=B)
                co = cos_sb[:, 0:SK].unsqueeze(1).broadcast_to([D, B, SK])
                si = sin_sb[:, 0:SK].unsqueeze(1).broadcast_to([D, B, SK])
                dve.tensor_tensor(k1[:, r, :].rearrange("p (b s) -> p b s", b=B), kin, co, ALU.mult)
                for lo in range(2):
                    ins = dve.tensor_tensor(k2[rows[lo], r, :].rearrange("p (b s) -> p b s", b=B), kin[rows[1 - lo]], si[rows[lo]], ALU.mult)
                ins.then_inc(krot, 1)
                dve.wait_ge(krot, g + 1)
                dve.tensor_tensor(k1[:, r, :], k1[:, r, :], k2[:, r, :], ALU.add).then_inc(kst, 1)

            for r in range(2):
                kv_rotate(0, r)
            with dve.Fori(1, NKV // 2) as i:
                for r in range(2):
                    kv_rotate(i, r)

            def norm(m, t, r):
                for half in range(2):
                    ins = dve.bn_stats(stats[:, r, half, :], acc[:, t, ts(half, HALF)])
                ins.then_inc(stat_done, 1)
                dve.wait_ge(stat_done, m + 1)
                dve.bn_aggr(mv[:, r, :], stats[:, r, :, :]).then_inc(aggr_done, 1)
                dve.wait_ge(rstd_done, m + 1)
                dve.tensor_scalar(qr[:, 2 * r:2 * r + 2, :].rearrange("p a q -> p (a q)"), acc[:, t, :],
                                  mv[:, r, 0:1], rstd[:, r, :], ALU.subtract, ALU.mult).then_inc(xn_done, 1)

            def norm_x(bp, i, r):
                q = i * 2 + r
                dve.wait_ge(s_x[q - bp * TP], 16 * (bp + 1))
                wait(dve, xt_done, q + bp * TP - 1)
                norm(q + bp * TP, q - bp * TP, r)
                for kh in range(2):
                    dve.wait_ge(xt_hi, q * 2 + kh + 1)
                    cols = ds((q - bp * TP) * P, P)
                    ins = dve.tensor_tensor(xl[:, 4 * kh:4 * kh + 4, cols], bank[2 * r + kh][:].rearrange("p (k t) -> p k t", k=4),
                                            xh[:, 4 * kh:4 * kh + 4, cols], ALU.subtract)
                ins.then_inc(xt_lo, 1)

            def rotate(n, u):
                j, b = u // 2, u % 2
                dve.wait_ge(q_done, n * 8 + u + 1)
                if j < 2:
                    wait(dve, s_done, n * 4 - 1 + b)
                else:
                    dve.wait_ge(s_done, n * 4 + b + 1)
                wait(dve, q_ready, n * 8 + u - 1)
                dve.tensor_tensor(qr[:, 2 * (j % 2) + b, :], q_ps[b][:], cos_sb[:], ALU.mult)
                dve.tensor_tensor(qt2[0:64, b, :], q_ps[b][64:128, :], sin_sb[0:64, :], ALU.mult)
                dve.tensor_tensor(qt2[64:128, b, :], q_ps[b][0:64, :], sin_sb[64:128, :], ALU.mult).then_inc(q_rot, 1)

            def mask_scores(m, c, b):
                s = m * 4 + (2 * c + b)
                dve.wait_ge(s_done, s + 1)
                wait(dve, t1_done, s)
                dve.tensor_tensor(soft[:, 0, 0:SK], st_ps[:, 0:SK], mask_sb[:], ALU.add).then_inc(st_mask, 1)

            def less_max(m, c, b):
                s = m * 4 + (2 * c + b)
                dve.wait_ge(t1_done, s + 1)
                sn = sn_ps[:].rearrange("p (g k) -> p g k", k=SK)
                dve.tensor_reduce(mx[:, b, :], sn, X, ALU.max).then_inc(mx_done, 1)
                dve.wait_ge(mx_done, s + 1)
                wait(dve, t2_done, s - 1)
                dve.tensor_tensor(soft[:, 1 + b, :].rearrange("p (g k) -> p g k", k=SK), sn,
                                  mx[:, b, :].unsqueeze(2).broadcast_to([P, 8, SK]), ALU.subtract).then_inc(sub_done, 1)

            def sums(m, c, b):
                s = m * 4 + (2 * c + b)
                dve.wait_ge(exp_done, s + 1)
                dve.tensor_reduce(sm[:, b, :], soft[:, 1 + b, :].rearrange("p (g k) -> p g k", k=SK), X, ALU.add).then_inc(sum_done, 1)
                dve.wait_ge(sum_done, s + 1)
                dve.reciprocal(rc[:, b, :], sm[:, b, :]).then_inc(rc_done, 1)

            def probs_low(m, c, b):
                s = m * 4 + (2 * c + b)
                dve.wait_ge(pt_hi, s + 1)
                dve.tensor_tensor(ptl[:, c, b, :], pt_ps[:], pth[:, c, b, :], ALU.subtract).then_inc(pt_lo, 1)

            def values_low(m, j):
                for half in range(2):
                    dve.wait_ge(vw_hi, m * 8 + 2 * j + half + 1)
                    ps = ov_ps[(2 * j + half) % 3]
                    for at in range(2):
                        rows, b = slice(64 * at, 64 * at + 64), at ^ (j % 2)
                        ins = dve.tensor_tensor(vwl[rows, j // 2, b, ts(half, HALF)], ps[rows, :], vwh[rows, j // 2, b, ts(half, HALF)], ALU.subtract)
                    ins.then_inc(ov_free, 1)

            def turn(n, g, prev, cur):
                m = n - 1
                for u in range(2 * HG):
                    if cur:
                        rotate(n, u)
                    if prev and u == 0:
                        mask_scores(m, 1, 1)
                        less_max(m, 1, 0)
                        values_low(m, 3)
                        sums(m, 1, 0)
                    if prev and u == 1:
                        less_max(m, 1, 1)
                        sums(m, 1, 1)
                    if prev and u == 2:
                        probs_low(m, 1, 0)
                    if prev and u == 3:
                        probs_low(m, 1, 1)
                    if cur and u == 3:
                        mask_scores(n, 0, 0)
                    if prev and u == 4:
                        for o in range(16):
                            b, q, half = o // 8, o // 2 % 4, o % 2
                            dve.wait_ge(ov_done, m * 24 + 8 + o + 1)
                            part = acc[:, b * QT + q, ts(half, HALF)]
                            dve.tensor_tensor(part, part, ov_ps[(8 + o) % 3][:], ALU.add).then_inc(ov_free, 1)
                    if not cur:
                        continue
                    if u == 4:
                        less_max(n, 0, 0)
                        mask_scores(n, 0, 1)
                        dve.wait_ge(v_hi, n + 1)
                        dve.tensor_tensor(vl[:], vraw[:], vh[:], ALU.subtract).then_inc(v_lo, 1)
                        sums(n, 0, 0)
                    if u == 5:
                        less_max(n, 0, 1)
                        values_low(n, 0)
                        sums(n, 0, 1)
                    if u == 6:
                        probs_low(n, 0, 0)
                        values_low(n, 1)
                    if u == 7:
                        probs_low(n, 0, 1)
                        values_low(n, 2)
                        mask_scores(n, 1, 0)


            def route(bp, t):
                i = bp * TP + t
                at = [i * CHAIN]

                def link(ins):
                    at[0] += 1
                    ins.then_inc(r_chain, 1)
                    dve.wait_ge(r_chain, at[0])

                dve.wait_ge(lg_done, i + 1)
                dve.tensor_copy(lgt[:], bank[4][0:NE, 0:P]).then_inc(lgt_done, 1)
                dve.wait_ge(lgn_done, i + 1)
                link(dve.tensor_copy(lg[:], bank[5][:, 0:NE]))
                link(dve.max(top[:], lg[:]))
                link(dve.max_index(top_i[:], top[:], lg[:]))
                link(dve.tensor_copy(top_f[:], top_i[:, 0:2]))
                dve.tensor_tensor(gap[:], top[:, 1:2], top[:, 0:1], ALU.subtract).then_inc(gap_done, 1)
                for k in range(2):
                    ins = dve.tensor_scalar(hot[:, k, :], iota_e[:], top_f[:, k:k + 1], None, ALU.is_equal)
                link(ins)
                dve.tensor_tensor(hot[:, 2, :], hot[:, 0, :], hot[:, 1, :], ALU.add).then_inc(hot_done, 1)
                dve.wait_ge(cnt_mm, i + 1)
                link(dve.tensor_tensor(pos[:], bank[6][:, 0:NE], count[:], ALU.add))
                link(dve.tensor_tensor(pick[:], hot[:, 0:2, :], pos[:].unsqueeze(1).broadcast_to([P, 2, NE]), ALU.mult))
                link(dve.tensor_reduce(pos_k[:], pick[:], X, ALU.add))
                link(dve.scalar_tensor_tensor(out=slot_f[:], in0=top_f[:], scalar=float(CAP), in1=pos_k[:], op0=ALU.mult, op1=ALU.add))
                for k in range(2):
                    wait(dve, s_scat[k], i * 16)
                dve.tensor_copy(slot_i[:], slot_f[:])
                link(dve.tensor_tensor(count[:], bank[6][:, NE:2 * NE], count[:], ALU.add))
                dve.wait_ge(egap_done, i + 1)
                link(dve.tensor_scalar(den[:], egap[:], 1.0, None, ALU.add))
                link(dve.reciprocal(den[:], den[:]))
                link(dve.tensor_tensor(w1[:], den[:], tanh_f[:], ALU.mult))
                dve.tensor_copy(pair[:, 0, 1:2], w1[:])
                dve.tensor_tensor(pair[:, 1, 1:2], w1[:], egap[:], ALU.mult)
                dve.tensor_scalar(pair[:, 0, 0:1], iota_p[:], float(i * P), None, ALU.add)
                link(dve.tensor_scalar(pair[:, 1, 0:1], iota_p[:], float(i * P), None, ALU.add))
                assert at[0] == (i + 1) * CHAIN

            for bp in range(BP):
                for t in range(TP):
                    norm_x(bp, bp * QT + t // 2, t % 2)
                turns(dve, bp, turn)
                for t in range(TP):
                    i = bp * TP + t
                    m = 2 * TP * bp + TP + t
                    if t >= 2:
                        dve.wait_ge(xt_done, m - 1)
                        dve.wait_ge(s_xn[t % 2], 16 * ((bp * TP + t) // 2))
                    norm(m, t, t % 2)
                    if t:
                        route(bp, t - 1)
                route(bp, TP - 1)
                for r in range(2):
                    dve.wait_ge(s_xn[r], 16 * (TP // 2) * (bp + 1))

            for t in range(TP):
                dve.wait_ge(s_x1[t], 16 * BP)
            at = [0]

            def link(ins):
                at[0] += 1
                ins.then_inc(e_chain, 1)
                dve.wait_ge(e_chain, at[0])

            link(dve.tensor_scalar(tile_n[:], count[:], float(P - 1), None, ALU.add))
            link(dve.tensor_scalar(tile_n[:], tile_n[:], P.bit_length() - 1, None, ALU.arith_shift_right))
            link(dve.tensor_scalar(tile_n[:], tile_n[:], 1.0, None, ALU.max))
            link(dve.tensor_copy(pre[:, 0, :], tile_n[:]))
            for k in range(4):
                a, b, by = k % 2, 1 - k % 2, 2 ** k
                dve.tensor_copy(pre[:, b, 0:by], pre[:, a, 0:by])
                link(dve.tensor_tensor(pre[:, b, by:NE], pre[:, a, by:NE], pre[:, a, 0:NE - by], ALU.add))
            dve.memset(tile_at[:, 0:1], 0)
            link(dve.tensor_copy(tile_at[:, 1:NE + 1], pre[:, 0, :]))
            for w in (guh, gul):
                ins = dve.memset(w[:, :, :, 2 * FI:GW].bitcast(f32), 0.0)
            ins.then_inc(pads, 1)
            dve.wait_ge(lists_done, 1)
            dve.tensor_copy(row_all[:], bank[4][:, 0:2 * P]).then_inc(rows_done, 1)
            dve.tensor_copy(w_all[:], bank[5][:, 0:2 * P]).then_inc(rows_done, 1)
            dve.wait_ge(rows_done, 2)
            dve.tensor_copy(w_of[:, 0:ET], w_all[:, 0:ET]).then_inc(w_chain, 1)
            with dve.Fori(1, NE) as e:
                t0 = dve.value_load(tile_at[0:1, ds(e, 1)], min_val=1, max_val=MT)
                dve.wait_ge(w_chain, e)
                dve.tensor_copy(w_of[:, ds(t0, ET)], w_all[:, ds(e * ET, ET)]).then_inc(w_chain, 1)
            dve.wait_ge(w_chain, NE)

            def split_low(e, r):
                dve.wait_ge(w_hi, e + 1)
                dve.tensor_tensor(gul[:, r, :, 0:2 * FI], gu_raw[:, r, :].rearrange("p (k n) -> p k n", k=KC), guh[:, r, :, 0:2 * FI], ALU.subtract)
                dve.tensor_tensor(dnl[:, r, :], dn_raw[:, r, :], dnh[:, r, :], ALU.subtract).then_inc(w_lo, 1)

            def rows_low(t, half):
                dve.wait_ge(xf_hi, t * 2 + half + 1)
                rows = slice(4 * half, 4 * half + 4)
                return dve.tensor_tensor(xfl[:, rows, :], xf_ps[half][:].rearrange("p (k t) -> p k t", k=4), xfh[:, rows, :], ALU.subtract)

            def inner(t):
                dve.wait_ge(silu_done, t)
                dve.scalar_tensor_tensor(out=hm[:], in0=sg[:], scalar=w_of[:, ds(t - 1, 1)], in1=gu_ps[:, FI:2 * FI], op0=ALU.mult, op1=ALU.mult).then_inc(h_done, 1)

            def inner_low(t):
                dve.wait_ge(ht_hi, t)
                dve.tensor_tensor(htl[:], ht_ps[0:FI, 0:P], hth[:], ALU.subtract).then_inc(ht_lo, 1)

            def out_b(t):
                dve.wait_ge(d_done, t)
                dve.wait_ge(s_add, t * 16 + 16)
                dve.tensor_copy(ys[:, HALF:C], y_ps[1][:]).then_inc(y_b, 1)

            def tile(t, r):
                inner(t)
                rows_low(t, 0)
                inner_low(t)
                rows_low(t, 1).then_inc(xf_lo, 1)
                out_b(t)

            def first(e, r, t, is_last):
                if isinstance(e, int) and e == 0:
                    rows_low(t, 0)
                    rows_low(t, 1).then_inc(xf_lo, 1)
                else:
                    tile(t, r)
                if not is_last:
                    split_low(e + 1, 1 - r)

            def tail(t):
                inner(t)
                inner_low(t)
                out_b(t)

            split_low(0, 0)
            experts(dve, tile, first, tail)

        @block.scalar
        def _(act):
            act.wait_ge(s_const, 16 * 8)
            act.activation(tanh_x[:], gates_raw[:, 0:1], ACT.Tanh).then_inc(tanh_done, 1)
            act.activation(tanh_f[:], gates_raw[:, 1:2], ACT.Tanh).then_inc(tanh_done, 1)
            act.wait_ge(tanh_done, 2)

            def kv_scale(i, r):
                act.wait_ge(vproj, i * 2 + r + 1)
                wait(act, s_kvout[2 + r], i * 16)
                act.activation(v1[:, r, :], bank[2 + r][:, 0:B * SK], ACT.Copy, scale=tanh_x[:, 0:1]).then_inc(vst, 1)

            for r in range(2):
                kv_scale(0, r)
            with act.Fori(1, NKV // 2) as i:
                for r in range(2):
                    kv_scale(i, r)

            def split_wq(n, u):
                h = n * 8 + u
                act.wait_ge(s_wq[u % 2], n * 64 + (u // 2) * 16 + 16)
                wait(act, q_done, n * 8 + u - u % 2 - 2)
                act.activation(wqh[:, u % 4, :], wq_raw[:, u % 2, :], ACT.Copy).then_inc(wq_hi, 1)

            def split_wd(n, u):
                act.wait_ge(s_wd[u % 2], n * 64 + (u // 2) * 16 + 16)
                wait(act, ov_done, n * 24 + u - 1 if u >= 2 else n * 24 - 17 + u)
                act.activation(wdh[:, u % 2, :], wd_raw[:, u % 2, :], ACT.Copy).then_inc(wd_hi, 1)

            def norm_x(bp, i, r):
                q = i * 2 + r
                act.wait_ge(xt_done, q + bp * TP + 1)
                for kh in range(2):
                    act.activation(xh[:, 4 * kh:4 * kh + 4, ds((q - bp * TP) * P, P)],
                                   bank[2 * r + kh][:].rearrange("p (k t) -> p k t", k=4), ACT.Copy).then_inc(xt_hi, 1)

            def copy_scores(m, c, b):
                s = m * 4 + (2 * c + b)
                act.wait_ge(st_mask, s + 1)
                act.activation(soft[:, 0, SK:S], st_ps[:, SK:S], ACT.Copy).then_inc(st_copy, 1)

            def exps(m, c, b):
                s = m * 4 + (2 * c + b)
                act.wait_ge(sub_done, s + 1)
                act.activation(soft[:, 1 + b, :], soft[:, 1 + b, :], ACT.Exp, scale=SCALE).then_inc(exp_done, 1)

            def probs_high(m, c, b):
                s = m * 4 + (2 * c + b)
                act.wait_ge(t2_done, s + 1)
                wait(act, ov_done, m * 24)
                act.activation(pth[:, c, b, :], pt_ps[:], ACT.Copy).then_inc(pt_hi, 1)

            def values_high(m, j):
                for half in range(2):
                    act.wait_ge(ov_done, m * 24 + 2 * j + half + 1)
                    ps = ov_ps[(2 * j + half) % 3]
                    for at in range(2):
                        rows, b = slice(64 * at, 64 * at + 64), at ^ (j % 2)
                        ins = act.activation(vwh[rows, j // 2, b, ts(half, HALF)], ps[rows, :], ACT.Copy)
                    ins.then_inc(vw_hi, 1)

            def turn(n, g, prev, cur):
                m = n - 1
                last = isinstance(n, int) and n == NG - 1
                for u in range(2 * HG):
                    if cur and u < 6:
                        split_wq(n, u + 2)
                    elif cur and not last:
                        split_wq(n + 1, u - 6)
                    if prev and u == 0:
                        split_wd(m, 6)
                        split_wd(m, 7)
                        copy_scores(m, 1, 1)
                        values_high(m, 3)
                        exps(m, 1, 0)
                    if prev and u == 1:
                        exps(m, 1, 1)
                    if prev and u == 2:
                        probs_high(m, 1, 0)
                    if prev and u == 3:
                        probs_high(m, 1, 1)
                    if not cur:
                        continue
                    if u == 3:
                        split_wd(n, 0)
                        copy_scores(n, 0, 0)
                    if u == 4:
                        split_wd(n, 1)
                        act.wait_ge(s_v, n * 32 + 32)
                        wait(act, ov_done, n * 24 - 16)
                        act.activation(vh[:], vraw[:], ACT.Copy).then_inc(v_hi, 1)
                        copy_scores(n, 0, 1)
                        exps(n, 0, 0)
                    if u == 5:
                        values_high(n, 0)
                        exps(n, 0, 1)
                    if u == 6:
                        split_wd(n, 2)
                        split_wd(n, 3)
                        probs_high(n, 0, 0)
                        values_high(n, 1)
                    if u == 7:
                        split_wd(n, 4)
                        split_wd(n, 5)
                        probs_high(n, 0, 1)
                        values_high(n, 2)
                        copy_scores(n, 1, 0)

            def route(bp, t):
                i = bp * TP + t
                act.wait_ge(gap_done, i + 1)
                act.activation(egap[:], gap[:], ACT.Exp).then_inc(egap_done, 1)

            def copy_tile(bp, t):
                i = bp * TP + t
                act.wait_ge(xt_done, 2 * TP * bp + TP + t + 1)
                if t:
                    act.wait_ge(lg_done, i)
                for kh in range(2):
                    ins = act.activation(xt2[:, 4 * kh:4 * kh + 4, :], bank[2 * (t % 2) + kh][:].rearrange("p (k t) -> p k t", k=4), ACT.Copy)
                ins.then_inc(xt2_done, 1)

            for u in range(2):
                split_wq(0, u)
            for bp in range(BP):
                if bp:
                    act.wait_ge(q_done, 8 * NKV * bp)
                for t in range(TP):
                    norm_x(bp, bp * QT + t // 2, t % 2)
                turns(act, bp, turn, last_apart=True)
                for t in range(TP):
                    copy_tile(bp, t)
                    if t:
                        route(bp, t - 1)
                route(bp, TP - 1)

            def split_high(e, r):
                act.wait_ge(s_gu[r], e // 2 * 16 + 16 if isinstance(e, int) else (e - r) * 8 + 16)
                act.activation(guh[:, r, :, 0:2 * FI], gu_raw[:, r, :].rearrange("p (k n) -> p k n", k=KC), ACT.Copy)
                act.wait_ge(s_dn[r], e // 2 * 16 + 16 if isinstance(e, int) else (e - r) * 8 + 16)
                act.activation(dnh[:, r, :], dn_raw[:, r, :], ACT.Copy).then_inc(w_hi, 1)

            def silu(t):
                act.wait_ge(gu_done, t)
                act.activation(sg[:], gu_ps[:, 0:FI], ACT.Silu).then_inc(silu_done, 1)

            def rows_high(t):
                act.wait_ge(tt_done, t + 1)
                for half in range(2):
                    act.activation(xfh[:, 4 * half:4 * half + 4, :], xf_ps[half][:].rearrange("p (k t) -> p k t", k=4), ACT.Copy).then_inc(xf_hi, 1)

            def inner_high(t):
                act.wait_ge(ht_done, t)
                act.activation(hth[:], ht_ps[0:FI, 0:P], ACT.Copy).then_inc(ht_hi, 1)

            def out_a(t):
                act.wait_ge(d_done, t)
                act.wait_ge(s_add, t * 16 + 16)
                act.activation(ys[:, 0:HALF], y_ps[0][:], ACT.Copy).then_inc(y_a, 1)

            def tile(t, r):
                silu(t)
                rows_high(t)
                inner_high(t)
                out_a(t)

            def first(e, r, t, is_last):
                if isinstance(e, int) and e == 0:
                    rows_high(t)
                else:
                    tile(t, r)
                if not is_last:
                    split_high(e + 1, 1 - r)

            def tail(t):
                silu(t)
                inner_high(t)
                out_a(t)

            act.wait_ge(pads, 1)
            split_high(0, 0)
            act.wait_ge(e_chain, E_CHAIN)
            experts(act, tile, first, tail)

        @block.gpsimd
        def _(pool):
            pool.memset(eps_half[:], -0.5).then_inc(iotas, 1)
            pool.iota(iota_e[:], [[1, NE]], base=0, channel_multiplier=0, allow_small_or_imprecise_dtypes=True).then_inc(iotas, 1)
            pool.iota(iota_p[:], [[0, 1]], base=0, channel_multiplier=1, allow_small_or_imprecise_dtypes=True).then_inc(iotas, 1)
            pool.iota(empty[:, :, 0], [[1, P]], base=T, channel_multiplier=0, allow_small_or_imprecise_dtypes=True).then_inc(iotas, 1)
            pool.memset(empty[:, :, 1], 0.0).then_inc(iotas, 1)
            pool.wait_ge(iotas, 5)
            for h in range(NE * ET // P):
                pool.dma_start(slots_hbm.rearrange("(a s) c -> a (s c)", s=P)[h * P:(h + 1) * P, :],
                               empty[:].rearrange("p s c -> p (s c)")).then_inc(s_slot0, 16)

            def split_wq(n, u):
                pool.wait_ge(wq_hi, n * 8 + u + 1)
                pool.tensor_tensor(wql[:, u % 4, :], wq_raw[:, u % 2, :], wqh[:, u % 4, :], ALU.subtract).then_inc(wq_lo, 1)

            def split_wd(n, u):
                pool.wait_ge(wd_hi, n * 8 + u + 1)
                pool.tensor_tensor(wdl[:, u % 2, :], wd_raw[:, u % 2, :], wdh[:, u % 2, :], ALU.subtract).then_inc(wd_lo, 1)

            def norm(m, r):
                pool.wait_ge(aggr_done, m + 1)
                pool.tensor_scalar(var_eps[:, r, :], mv[:, r, 1:2], EPS, None, ALU.add).then_inc(var_done, 1)
                pool.wait_ge(var_done, m + 1)
                pool.tensor_tensor(rstd[:, r, :], var_eps[:, r, :], eps_half[:], ALU.pow).then_inc(rstd_done, 1)

            def add_halves(n, u):
                slot = 2 * (u // 2 % 2) + u % 2
                pool.wait_ge(q_rot, n * 8 + u + 1)
                pool.tensor_tensor(qr[:, slot, :], qr[:, slot, :], qt2[:, u % 2, :], ALU.add).then_inc(q_ready, 1)

            def probs(m, c, b):
                s = m * 4 + (2 * c + b)
                pool.wait_ge(rc_done, s + 1)
                part = soft[:, 1 + b, :].rearrange("p (g k) -> p g k", k=SK)
                pool.tensor_tensor(part, part, rc[:, b, :].unsqueeze(2).broadcast_to([P, 8, SK]), ALU.mult).then_inc(p_done, 1)

            def turn(n, g, prev, cur):
                m = n - 1
                last = isinstance(n, int) and n == NG - 1
                for u in range(2 * HG):
                    if cur and u < 6:
                        split_wq(n, u + 2)
                    elif cur and not last:
                        split_wq(n + 1, u - 6)
                    if prev and u == 0:
                        split_wd(m, 6)
                        split_wd(m, 7)
                    if prev and u == 1:
                        probs(m, 1, 0)
                    if prev and u == 2:
                        probs(m, 1, 1)
                    if not cur:
                        continue
                    for d in {3: (0,), 4: (1,), 6: (2, 3), 7: (4, 5)}.get(u, ()):
                        split_wd(n, d)
                    if u == 5:
                        probs(n, 0, 0)
                    if u == 6:
                        probs(n, 0, 1)
                    add_halves(n, u)

            for u in range(2):
                split_wq(0, u)
            for bp in range(BP):
                for t in range(TP):
                    norm(2 * TP * bp + t, t % 2)
                turns(pool, bp, turn, last_apart=True)
                for t in range(TP):
                    norm(2 * TP * bp + TP + t, t % 2)
                    if t:
                        scatter_slots(pool, bp * TP + t - 1)
                scatter_slots(pool, bp * TP + TP - 1)

            for t in range(TP):
                pool.wait_ge(s_x1[t], 16 * BP)
            pool.memset(ys[:, 0:HALF], 0.0).then_inc(y_a, 1)
            pool.memset(ys[:, HALF:C], 0.0).then_inc(y_b, 1)
            pool.wait_ge(y_a, 1)
            pool.wait_ge(y_b, 1)
            pool.dma_start(xn_hbm[T:T + P, :], ys[:]).then_inc(s_add, 16)
            pool.wait_ge(s_add, 16)
            pool.dma_start(out[T:T + P, :], ys[:]).then_inc(s_add, 16)
            pool.wait_ge(rows_done, 2)
            pool.wait_ge(e_chain, E_CHAIN)
            pool.tensor_copy(row_of[:, 0:ET], row_all[:, 0:ET]).then_inc(rows_chain, 1)
            with pool.Fori(1, NE) as e:
                t0 = pool.value_load(tile_at[0:1, ds(e, 1)], min_val=1, max_val=MT)
                pool.wait_ge(rows_chain, e)
                pool.tensor_copy(row_of[:, ds(t0, ET)], row_all[:, ds(e * ET, ET)]).then_inc(rows_chain, 1)
            pool.wait_ge(rows_chain, NE)
            for r in range(2):
                pool.wait_ge(s_xn[r], 16 * (TP // 2) * BP)
            total = pool.value_load(tile_at[0:1, NE:NE + 1], min_val=NE, max_val=MT)

            def gather(t):
                if not (isinstance(t, int) and t == 0):
                    pool.wait_ge(s_gather, t * 16)
                    pool.wait_ge(tt_done, t)
                pool.tensor_copy(row_g[:], row_of[:, ds(t, 1)])
                pool.drain()
                pool.indirect_dma_start(out=xg[:], out_offset=None, in_=xn_hbm,
                                        in_offset=bass.IndirectOffsetOnAxis(ap=row_g[:, 0:1], axis=0)).then_inc(s_gather, 16)

            def scatter(t):
                pool.wait_ge(y_a, t)
                pool.wait_ge(y_b, t)
                pool.wait_ge(s_add, t * 16)
                pool.tensor_copy(row_s[:], row_of[:, ds(t - 2, 1)])
                pool.drain()
                pool.indirect_dma_start(out=out, out_offset=bass.IndirectOffsetOnAxis(ap=row_s[:, 0:1], axis=0),
                                        in_=ys[:], in_offset=None, compute_op=ALU.add).then_inc(s_add, 16)

            gather(0)
            gather(1)
            with pool.Fori(2, total) as t:
                gather(t)
                scatter(t)
            scatter(total)
            scatter(total + 1)
            pool.wait_ge(s_add, total * 16 + 32)


def _tables():
    inv = (1.0 / (np.float32(10000.0) ** (np.arange(0, D, 2, dtype=np.float32) / np.float32(D)))).astype(np.float32)
    ang = (np.arange(S, dtype=np.float32)[:, None] * inv[None, :]).astype(np.float32)
    c, s = np.cos(ang).astype(np.float32).T, np.sin(ang).astype(np.float32).T
    key, query = np.arange(P)[:, None] % SK, np.arange(SK)[None, :]
    return {
        "cos": np.ascontiguousarray(np.concatenate([c, c], 0)),
        "sin": np.ascontiguousarray(np.concatenate([-s, s], 0)),
        "mask": np.where(key <= query, 0.0, MASKED).astype(np.float32),
        "ident": np.eye(P, dtype=np.float32),
        "tri": np.triu(np.ones((P, P), np.float32), 1),
    }


def kernel(x, ctx_4096, g_xattn, g_ffn, L0_xattn_Wq, L0_xattn_Wk, L0_xattn_Wv, L0_xattn_Wd, L0_ffn_gate_w, L0_ffn_u, L0_ffn_g, L0_ffn_d):
    import concourse.bacc as bacc
    from concourse.bass_utils import run_bass_kernel_spmd

    def lay(a, *order_shape):
        return np.ascontiguousarray(a)

    x, ctx = np.asarray(x), np.asarray(ctx_4096)
    wq, wk, wv, wd = (np.asarray(a) for a in (L0_xattn_Wq, L0_xattn_Wk, L0_xattn_Wv, L0_xattn_Wd))
    gate, u, g, d = (np.asarray(a) for a in (L0_ffn_gate_w, L0_ffn_u, L0_ffn_g, L0_ffn_d))

    def by_head(w, heads):
        return lay(w.reshape(heads, D, KC, P).transpose(0, 3, 2, 1).reshape(heads, P, KC * D))

    arrays = {
        "x": lay(x.reshape(T, C)),
        "ctx_t": lay(ctx.reshape(B * SK, KC, P).transpose(2, 1, 0)),
        "g_x": lay(np.asarray(g_xattn).reshape(1)),
        "g_f": lay(np.asarray(g_ffn).reshape(1)),
        "wq": by_head(wq, NH),
        "wk": by_head(wk, NKV),
        "wv": by_head(wv, NKV),
        "wd": lay(wd.reshape(C, NH, D).transpose(1, 2, 0)),
        "gate": lay(gate.reshape(NE, KC, P).transpose(2, 1, 0)),
        "gu": lay(np.stack([g.reshape(NE, FI, KC, P), u.reshape(NE, FI, KC, P)], 1).transpose(0, 4, 3, 1, 2).reshape(NE, P, KC, 2 * FI)),
        "dn": lay(d.reshape(C, NE, FI).transpose(1, 2, 0)),
        **_tables(),
    }
    nc = bacc.Bacc("TRN2", target_bir_lowering=False, num_devices=1)
    args = {n: nc.dram_tensor(f"{n}_dram", a.shape, mybir.dt.from_np(a.dtype), kind="ExternalInput").ap() for n, a in arrays.items()}
    out = nc.dram_tensor("out_dram", (T + P, C), mybir.dt.float32, kind="ExternalOutput").ap()
    program(nc, out=out, **args)
    r = run_bass_kernel_spmd(nc, [{f"{n}_dram": a for n, a in arrays.items()}], core_ids=[0])
    return r.results[0]["out_dram"][:T].reshape(B, S, C)
```

```python
import numpy as np
import concourse.bass as bass
from concourse import mybir
from contextlib import ExitStack

B, S, C = 4, 512, 1024
SK = 64
NH, NKV, D = 32, 8, 128
NE, FI = 16, 112
P = 128
T = B * S
KC = C // P
BP = B // 2
HG = NH // NKV
NG = BP * NKV
QT = S // P
TP = 2 * QT
HALF = C // 2
CAP = T
ET = CAP // P
MT = 2 * T // P + NE
SCALE = float(D) ** -0.5
EPS = 1e-5
MASKED = -2.0 ** 127
GW = 256
E_CHAIN = 9
RB = QT
NR = B * QT // RB
X_LAG = 3


def program(nc, x, ctx_t, g_x, g_f, wq, wk, wv, wd, gate, gu, dn, cos, sin, mask, ident, tri, out):
    f32, f32r, i32, u32 = mybir.dt.float32, mybir.dt.float32r, mybir.dt.int32, mybir.dt.uint32
    ALU, ACT, X = mybir.AluOpType, mybir.ActivationFunctionType, mybir.AxisListType.X

    keep = ExitStack()
    with keep:
        def sem(name):
            return keep.enter_context(nc.semaphore(name))

        def sb(stack, name, shape, dt=f32):
            return stack.enter_context(nc.sbuf_tensor(name, shape, dt))

        ds, ts = bass.ds, bass.ts

        def wait(eng, s, value):
            if not isinstance(value, int) or value > 0:
                eng.wait_ge(s, value)

        k_hbm = nc.dram_tensor("k_hbm", (NKV, D, B * SK), f32).ap()
        v_hbm = nc.dram_tensor("v_hbm", (NKV, D, B * SK), f32).ap()
        xn_hbm = nc.dram_tensor("xn_hbm", (T + P, C), f32).ap()
        slots_hbm = nc.dram_tensor("slots_hbm", (NE * CAP, 2), f32).ap()

        idn = sb(keep, "idn", [P, P])
        tri_sb = sb(keep, "tri_sb", [P, P])
        ones = sb(keep, "ones", [P, P])
        eps_half = sb(keep, "eps_half", [P, 1])
        tanh_x = sb(keep, "tanh_x", [P, 1])
        tanh_f = sb(keep, "tanh_f", [P, 1])
        gates_raw = sb(keep, "gates_raw", [P, 2])
        before = sb(keep, "before", [P, B * QT + 1, NE])
        tile_n = sb(keep, "tile_n", [P, NE], i32)
        tile_at = sb(keep, "tile_at", [P, NE + 1], i32)

        bank = [keep.enter_context(nc.psum_tensor(f"bank{i}", [P, 512], f32)) for i in range(8)]
        q_ps = bank[0:2]
        st_ps = bank[2]
        sn_ps = bank[3]
        pt_ps = bank[4]
        ov_ps = bank[5:8]

        att = ExitStack()
        xh = sb(att, "xh", [P, KC, 2 * S], f32r)
        xl = sb(att, "xl", [P, KC, 2 * S], f32r)
        acc = sb(att, "acc", [P, TP, C])
        kcur = sb(att, "kcur", [P, 2 * SK])
        vraw = sb(att, "vraw", [P, 3 * SK])
        vh = sb(att, "vh", [P, 3 * SK], f32r)
        vl = sb(att, "vl", [P, 3 * SK], f32r)
        wq_raw = sb(att, "wq_raw", [P, 2, HALF])
        wqh = sb(att, "wqh", [P, 4, HALF], f32r)
        wql = sb(att, "wql", [P, 4, HALF], f32r)
        wd_raw = sb(att, "wd_raw", [P, 2, HALF])
        wdh = sb(att, "wdh", [P, 2, HALF], f32r)
        wdl = sb(att, "wdl", [P, 2, HALF], f32r)
        cos_sb = sb(att, "cos_sb", [P, S])
        sin_sb = sb(att, "sin_sb", [P, S])
        mask_sb = sb(att, "mask_sb", [P, SK])
        qr = sb(att, "qr", [P, 4, S])
        qt2 = sb(att, "qt2", [P, 2, S])
        soft = sb(att, "soft", [P, 3, S])
        mx = sb(att, "mx", [P, 2, 8])
        sm = sb(att, "sm", [P, 2, 8])
        rc = sb(att, "rc", [P, 2, 8])
        stats = sb(att, "stats", [P, 2, 2, 2, 6])
        mv = sb(att, "mv", [P, 2, 2, 2])
        var_eps = sb(att, "var_eps", [P, 2, 2, 1])
        rstd = sb(att, "rstd", [P, 2, 2, 1])
        gate_sb = sb(att, "gate_sb", [P, KC, NE])
        xt2 = [a.rearrange("p a q -> p (a q)").rearrange("p (k t) -> p k t", k=KC) for a in (soft[:, 0:2, :], qt2[:])]
        lg = sb(att, "lg", [P, RB, NE])
        top = sb(att, "top", [P, RB, 8])
        top_i = sb(att, "top_i", [P, RB, 8], u32)
        top_f = sb(att, "top_f", [P, 2, RB])
        iota_e = sb(att, "iota_e", [P, NE])
        token = sb(att, "token", [P, NR, RB])
        hot = sb(att, "hot", [P, 3, RB * NE])
        pos = sb(att, "pos", [P, RB * NE])
        pick = sb(att, "pick", [P, 2, RB * NE])
        pos_k = sb(att, "pos_k", [P, 2, RB])
        slot_f = sb(att, "slot_f", [P, 2, RB])
        slot_i = sb(att, "slot_i", [P, NR, 2, RB], i32)
        gap = sb(att, "gap", [P, RB])
        egap = sb(att, "egap", [P, RB])
        den = sb(att, "den", [P, RB])
        w1 = sb(att, "w1", [P, RB])
        entry = sb(att, "entry", [P, NR, 2, RB, 2])

        early = ExitStack()
        ctx_sb = sb(early, "ctx_sb", [P, KC, B * SK])
        wkv = sb(early, "wkv", [P, 4, KC * D])
        k1 = sb(early, "k1", [P, 2, B * SK])
        k2 = sb(early, "k2", [P, 2, B * SK])
        v1 = sb(early, "v1", [P, 2, B * SK])
        empty = sb(early, "empty", [P, P, 2])
        early.close()
        pth = sb(att, "pth", [P, 2, 2, S], f32r)
        ptl = sb(att, "ptl", [P, 2, 2, S], f32r)
        vwh = sb(att, "vwh", [P, 2, 2, C], f32r)
        vwl = sb(att, "vwl", [P, 2, 2, C], f32r)
        att.close()

        ffn = ExitStack()
        gu_raw = sb(ffn, "gu_raw", [P, 2, KC * 2 * FI])
        guh = sb(ffn, "guh", [P, 2, KC, GW], f32r)
        gul = sb(ffn, "gul", [P, 2, KC, GW], f32r)
        dn_raw = sb(ffn, "dn_raw", [FI, 2, C])
        dnh = sb(ffn, "dnh", [FI, 2, C], f32r)
        over_acc = sb(ffn, "over_acc", [P, C // 2])
        dnl = sb(ffn, "dnl", [FI, 2, C], f32r)
        xg = sb(ffn, "xg", [P, C])
        xfh = sb(ffn, "xfh", [P, KC, P], f32r)
        xfl = sb(ffn, "xfl", [P, KC, P], f32r)
        sg = sb(ffn, "sg", [P, FI])
        hm = sb(ffn, "hm", [P, FI])
        hth = sb(ffn, "hth", [FI, P], f32r)
        htl = sb(ffn, "htl", [FI, P], f32r)
        ys = sb(ffn, "ys", [P, C])
        lists = sb(ffn, "lists", [P, 2, 2 * P])
        row_all = sb(ffn, "row_all", [P, NE * ET], i32)
        w_all = sb(ffn, "w_all", [P, NE * ET])
        row_of = sb(ffn, "row_of", [P, MT + ET], i32)
        w_of = sb(ffn, "w_of", [P, MT + ET])
        row_g = sb(ffn, "row_g", [P, 1], i32)
        row_s = sb(ffn, "row_s", [P, 1], i32)
        pre = sb(ffn, "pre", [P, 2, NE])
        ffn.close()

        s_const = sem("s_const")
        s_ctx = sem("s_ctx")
        s_kw = [sem(f"s_kw{i}") for i in range(4)]
        s_kvout = [sem(f"s_kvout{i}") for i in range(4)]
        s_x = [sem(f"s_x{i}") for i in range(TP)]
        s_wq = [sem(f"s_wq{i}") for i in range(2)]
        s_wd = [sem(f"s_wd{i}") for i in range(2)]
        s_k = sem("s_k")
        s_v = sem("s_v")
        s_x1 = [sem(f"s_x1_{i}") for i in range(TP)]
        s_xn = [sem(f"s_xn{i}") for i in range(TP)]
        s_zero = sem("s_zero")
        s_slot0 = sem("s_slot0")
        s_scat = [sem(f"s_scat{i}") for i in range(2)]
        setup = sem("setup")
        tanh_done = sem("tanh_done")
        iotas = sem("iotas")
        kproj, vproj = sem("kproj"), sem("vproj")
        krot, kst, vst = sem("krot"), sem("kst"), sem("vst")
        stat_done, aggr_done, var_done, rstd_done, xn_done, xt_done = (
            [sem(f"{n}{w + 1}") for w in range(2)] for n in ("stat_done", "aggr_done", "var_done", "rstd_done", "xn_done", "xt_done"))
        xt_hi, xt_lo = sem("xt_hi"), sem("xt_lo")
        wq_hi, wq_lo, wd_hi, wd_lo = (sem(n) for n in ("wq_hi", "wq_lo", "wd_hi", "wd_lo"))
        v_hi, v_lo = sem("v_hi"), sem("v_lo")
        q_done, q_rot, q_ready = sem("q_done"), sem("q_rot"), sem("q_ready")
        s_done, st_mask, st_copy = sem("s_done"), sem("st_mask"), sem("st_copy")
        t1_done, mx_done, sub_done, exp_done = (sem(n) for n in ("t1_done", "mx_done", "sub_done", "exp_done"))
        sum_done, rc_done, p_done = sem("sum_done"), sem("rc_done"), sem("p_done")
        t2_done, pt_hi, pt_lo = sem("t2_done"), sem("pt_hi"), sem("pt_lo")
        ov_done, vw_hi, ov_free = sem("ov_done"), sem("vw_hi"), sem("ov_free")
        xt2_done, lg_done, lg_taken = sem("xt2_done"), sem("lg_done"), sem("lg_taken")
        r_chain, gap_done, egap_done = sem("r_chain"), sem("gap_done"), sem("egap_done")
        hot_done, cnt_mm, routed = sem("hot_done"), sem("cnt_mm"), sem("routed")

        s_gu = [sem(f"s_gu{i}") for i in range(2)]
        s_dn = [sem(f"s_dn{i}") for i in range(2)]
        s_lists, s_gather, s_add = sem("s_lists"), sem("s_gather"), sem("s_add")
        lists_done, rows_done = sem("lists_done"), sem("rows_done")
        e_chain = sem("e_chain")
        w_hi, w_lo, pads = sem("w_hi"), sem("w_lo"), sem("pads")
        rows_chain, w_chain = sem("rows_chain"), sem("w_chain")
        g_set, g_seen, s_set, s_seen = sem("g_set"), sem("g_seen"), sem("s_set"), sem("s_seen")
        tt_done, xf_hi, xf_lo, gu_done = sem("tt_done"), sem("xf_hi"), sem("xf_lo"), sem("gu_done")
        silu_done, h_done, ht_done, ht_hi, ht_lo = (sem(n) for n in ("silu_done", "h_done", "ht_done", "ht_hi", "ht_lo"))
        d_done, y_a, y_b = sem("d_done"), sem("y_a"), sem("y_b")
        xf_ps, gu_ps, ht_ps, y_ps = bank[0:2], bank[2], bank[3], bank[4:6]


        block = keep.enter_context(nc.Block())


        def turns(eng, bp, turn, last_apart=False):
            turn(bp * NKV, 0, False, True)
            end = NKV - 1 if last_apart else NKV
            with eng.Fori(1, end) as g:
                turn(g + bp * NKV, g, True, True)
            if last_apart:
                turn(bp * NKV + NKV - 1, NKV - 1, True, True)
            turn(bp * NKV + NKV, NKV, True, False)


        STEPS_IN = TP + 3
        STEPS_OUT = TP + 3 + X_LAG


        def experts(eng, tile, first, tail):
            def expert(e, r, is_first, is_last):
                t0 = 0 if is_first else eng.value_load(tile_at[0:1, ds(e, 1)], min_val=1, max_val=MT)
                t1 = eng.value_load(tile_at[0:1, ds(e + 1, 1)], min_val=1, max_val=MT)
                first(e, r, t0, is_last)
                with eng.If(t1 > t0 + 1):
                    with eng.Fori(t0 + 1, t1) as t:
                        tile(t, r)

            expert(0, 0, True, False)
            expert(1, 1, False, False)
            with eng.Fori(1, NE // 2 - 1) as ep:
                for r in range(2):
                    expert(ep * 2 + r, r, False, False)
            expert(NE - 2, 0, False, False)
            expert(NE - 1, 1, False, True)
            tail(eng.value_load(tile_at[0:1, NE:NE + 1], min_val=NE, max_val=MT))

        @block.sync
        def _(sp):
            sp.dma_start(ctx_sb[:], ctx_t).then_inc(s_ctx, 16)
            sp.dma_start(gates_raw[:, 0:1], g_x.partition_broadcast(P)).then_inc(s_const, 16)
            sp.dma_start(gates_raw[:, 1:2], g_f.partition_broadcast(P)).then_inc(s_const, 16)
            sp.dma_start(cos_sb[:], cos).then_inc(s_const, 16)
            sp.dma_start(sin_sb[:], sin).then_inc(s_const, 16)

            def kv_weights(g, r):
                sp.dma_start(wkv[:, r, :], wk[g]).then_inc(s_kw[r], 16)
                sp.dma_start(wkv[:, 2 + r, :], wv[g]).then_inc(s_kw[2 + r], 16)

            def kv_store(g, r):
                sp.wait_ge(kst, g + 1)
                sp.dma_start(k_hbm[g], k1[:, r, :]).then_inc(s_kvout[r], 16)
                sp.wait_ge(vst, g + 1)
                sp.dma_start(v_hbm[g], v1[:, r, :]).then_inc(s_kvout[2 + r], 16)

            def load_x(bp, t):
                row = (bp * TP + t) * P
                sp.dma_start(acc[:, t, :], x[row:row + P, :]).then_inc(s_x[t], 16)

            for r in range(2):
                kv_weights(r, r)
                load_x(0, r)
            sp.dma_start(idn[:], ident).then_inc(s_const, 16)
            sp.dma_start(mask_sb[:], mask).then_inc(s_const, 16)
            sp.dma_start(tri_sb[:], tri).then_inc(s_const, 16)
            sp.dma_start(gate_sb[:], gate).then_inc(s_const, 16)
            for g in range(NKV):
                if g + 2 < NKV:
                    sp.wait_ge(vproj, g + 1)
                    kv_weights(g + 2, g % 2)
                if g + 2 < TP:
                    load_x(0, g + 2)
                kv_store(g, g % 2)

            def load_wq(n, head, u):
                wait(sp, wq_lo, n * 8 + u - 1)
                sp.dma_start(wq_raw[:, u % 2, :], wq[head, :, (u % 2) * HALF:(u % 2 + 1) * HALF]).then_inc(s_wq[u % 2], 16)

            def load_wd(n, head, u):
                wait(sp, wd_lo, n * 8 + u - 1)
                sp.dma_start(wd_raw[:, u % 2, :], wd[head, :, (u % 2) * HALF:(u % 2 + 1) * HALF]).then_inc(s_wd[u % 2], 16)

            def expert_weights(e, r):
                sp.dma_start(gu_raw[:, r, :], gu[e]).then_inc(s_gu[r], 16)
                sp.dma_start(dn_raw[:, r, :], dn[e]).then_inc(s_dn[r], 16)

            for u in range(2):
                load_wq(0, 0, u)

            for bp in range(BP):
                if bp == 0:
                    for r in range(4):
                        sp.wait_ge(s_kvout[r], 16 * (NKV // 2))

                def turn(n, g, prev, cur):
                    last = isinstance(n, int) and n == NG - 1
                    for u in range(2 * HG):
                        if cur and u < 6:
                            load_wq(n, g * HG + (u + 2) // 2, u + 2)
                        elif cur and not last:
                            nxt = 0 if isinstance(g, int) and g == NKV - 1 else g * HG + HG
                            load_wq(n + 1, nxt, u - 6)
                        if u == 0 and prev:
                            for d in (6, 7):
                                load_wd(n - 1, g * HG - 1, d)
                        if not cur:
                            continue
                        if u == 1:
                            wait(sp, s_done, n * 4)
                            sp.dma_start(kcur[:], k_hbm[g, :, bp * 2 * SK:(bp + 1) * 2 * SK]).then_inc(s_k, 16)
                            wait(sp, v_lo, n)
                            sp.dma_start(vraw[:, 0:2 * SK], v_hbm[g, :, bp * 2 * SK:(bp + 1) * 2 * SK]).then_inc(s_v, 16)
                            sp.dma_start(vraw[:, 2 * SK:3 * SK], v_hbm[g, :, bp * 2 * SK:bp * 2 * SK + SK]).then_inc(s_v, 16)
                        for d in {3: (0,), 4: (1,), 6: (2, 3), 7: (4, 5)}.get(u, ()):
                            load_wd(n, g * HG + d // 2, d)

                turns(sp, bp, turn, last_apart=True)

                if bp == BP - 1:
                    sp.wait_ge(q_done, 8 * NG)
                    for r in range(2):
                        expert_weights(r, r)
                for s in range(STEPS_OUT):
                    if s < TP:
                        sp.wait_ge(ov_free, 24 * (bp * NKV + NKV - 1) + 8 + 2 * s + 2)
                        row = (bp * TP + s) * P
                        sp.dma_start(out[row:row + P, :], acc[:, s, :]).then_inc(s_x1[s], 16)
                    if 0 <= s - 1 < TP:
                        t = s - 1
                        row = (bp * TP + t) * P
                        sp.wait_ge(xn_done[1], bp * TP + t + 1)
                        sp.dma_start(xn_hbm[row:row + P, :], acc[:, t, :]).then_inc(s_xn[t], 16)
                    if 0 <= s - 2 < TP and bp < BP - 1:
                        t = s - 2
                        sp.wait_ge(s_xn[t], 16 * (bp + 1))
                        sp.wait_ge(xt_done[1], bp * TP + t + 1)
                        load_x(bp + 1, t)

            for k in range(2):
                sp.wait_ge(s_scat[k], 16 * TP * BP)
            for t in range(TP):
                sp.wait_ge(s_x1[t], 16 * BP)
            for t in range(TP):
                sp.wait_ge(s_xn[t], 16 * BP)
            sp.dma_start(lists[:], slots_hbm.rearrange("(h a s) c -> a h (s c)", h=2, s=P)).then_inc(s_lists, 16)

            with sp.Fori(1, NE // 2) as ep:
                for r in range(2):
                    sp.wait_ge(w_lo, ep * 2 - 1 + r)
                    expert_weights(ep * 2 + r, r)

        @block.tensor
        def _(pe):
            pe.wait_ge(s_ctx, 16)

            def kv_project(g):
                r = g % 2
                for w, (taken, done) in enumerate(((krot, kproj), (vst, vproj))):
                    pe.wait_ge(s_kw[2 * w + r], g // 2 * 16 + 16)
                    wait(pe, taken, g - 1)
                    for k in range(KC):
                        mm = pe.matmul(bank[4 + 2 * w + r][:, 0:B * SK], wkv[:, 2 * w + r, k * D:(k + 1) * D], ctx_sb[:, k, :], start=(k == 0), stop=(k == KC - 1))
                    mm.then_inc(done, 1)

            def turn_x(bp, t):
                pe.wait_ge(xn_done[0], bp * TP + t + 1)
                wait(pe, xt_lo, bp * TP + t)
                for k in range(KC):
                    mm = pe.transpose(bank[2 + k // 4][:, ts(k % 4, P)], qr[:, 2 * (t % 2) + k // 4, ts(k % 4, P)], idn[:])
                mm.then_inc(xt_done[0], 1)

            def turn_x1(bp, t):
                pe.wait_ge(xn_done[1], bp * TP + t + 1)
                wait(pe, xt2_done, bp * TP + t)
                for k in range(KC):
                    mm = pe.transpose(bank[k // 4][:, ts(k % 4, P)], acc[:, t, ts(k, P)], idn[:])
                mm.then_inc(xt_done[1], 1)

            def logits(bp, t):
                pe.wait_ge(xt2_done, bp * TP + t + 1)
                if t % RB == 0:
                    wait(pe, lg_taken, bp * TP // RB + t // RB)
                for k in range(KC):
                    mm = pe.matmul(bank[4][:, ts(t, NE)], xt2[t % 2][:, k, :], gate_sb[:, k, :], start=(k == 0), stop=(k == KC - 1))
                mm.then_inc(lg_done, 1)

            def counts(q):
                pe.wait_ge(hot_done, q + 1)
                pe.wait_ge(ov_free, 24 * NKV * (q * RB // TP + 1))
                ps = ov_ps[q % (TP // RB)]
                pe.matmul(ps[:, 0:RB * NE], tri_sb[:], hot[:, 2, :], start=True, stop=True)
                pe.matmul(ps[:, RB * NE:2 * RB * NE], ones[:], hot[:, 2, :], start=True, stop=True).then_inc(cnt_mm, 1)

            def q_unit(n, u):
                j, b = u // 2, u % 2
                wait(pe, q_rot, n * 8 + u - 1)
                for kh in range(2):
                    if b == 0:
                        pe.wait_ge(wq_lo, n * 8 + 2 * j + kh + 1)
                    slot = (2 * j + kh) % 4
                    for kk in range(4):
                        k = 4 * kh + kk
                        cols = slice(b * S, (b + 1) * S)
                        pe.matmul(q_ps[b][:], wqh[:, slot, ts(kk, D)], xh[:, k, cols], start=(k == 0), stop=False)
                        pe.matmul(q_ps[b][:], wqh[:, slot, ts(kk, D)], xl[:, k, cols], start=False, stop=False)
                        mm = pe.matmul(q_ps[b][:], wql[:, slot, ts(kk, D)], xh[:, k, cols], start=False, stop=(k == KC - 1))
                mm.then_inc(q_done, 1)

            def scores(m, c, b):
                s = 4 * m + 2 * c + b if isinstance(m, int) else m * 4 + (2 * c + b)
                pe.wait_ge(q_ready, m * 8 + 4 * c + 2 + b + 1)
                pe.wait_ge(s_k, m * 16 + 16)
                wait(pe, st_copy, s)
                wait(pe, st_mask, s)
                for hh in range(2):
                    at = SK * (hh ^ b)
                    mm = pe.matmul(st_ps[at:at + SK, :], kcur[:, ts(b, SK)], qr[:, 2 * hh + b, :], start=True, stop=True)
                mm.then_inc(s_done, 1)

            def turn_scores(m, c, b):
                s = m * 4 + (2 * c + b)
                pe.wait_ge(st_copy, s + 1)
                pe.wait_ge(st_mask, s + 1)
                wait(pe, sub_done, s)
                for q in range(QT):
                    mm = pe.transpose(sn_ps[:, ts(q, P)], soft[:, 0, ts(q, P)], idn[:])
                mm.then_inc(t1_done, 1)

            def turn_probs(m, c, b):
                s = m * 4 + (2 * c + b)
                pe.wait_ge(p_done, s + 1)
                wait(pe, pt_lo, s)
                for q in range(QT):
                    mm = pe.transpose(pt_ps[:, ts(q, P)], soft[:, 1 + b, ts(q, P)], idn[:])
                mm.then_inc(t2_done, 1)

            def values_out(m, j):
                pe.wait_ge(v_lo, m + 1)
                cols = slice(0, 2 * SK) if j % 2 == 0 else slice(SK, 3 * SK)
                for half in range(2):
                    pe.wait_ge(wd_lo, m * 8 + 2 * j + half + 1)
                    wait(pe, ov_free, m * 24 + 2 * j + half - 2)
                    ps = ov_ps[(2 * j + half) % 3]
                    pe.matmul(ps[:], vh[:, cols], wdh[:, half, :], start=True, stop=False)
                    pe.matmul(ps[:], vh[:, cols], wdl[:, half, :], start=False, stop=False)
                    pe.matmul(ps[:], vl[:, cols], wdh[:, half, :], start=False, stop=True).then_inc(ov_done, 1)

            def output(m, o):
                b, q, half = o // 8, o // 2 % 4, o % 2
                pe.wait_ge(ov_free, m * 24 + max(8, 8 + o - 2))
                ps = ov_ps[(8 + o) % 3]
                for c in range(2):
                    ph, pl = pth[:, c, b, ts(q, P)], ptl[:, c, b, ts(q, P)]
                    wh, wl = vwh[:, c, b, ts(half, HALF)], vwl[:, c, b, ts(half, HALF)]
                    pe.matmul(ps[:], ph, wh, start=(c == 0), stop=False)
                    pe.matmul(ps[:], ph, wl, start=False, stop=False)
                    mm = pe.matmul(ps[:], pl, wh, start=False, stop=(c == 1))
                mm.then_inc(ov_done, 1)

            def turn(n, g, prev, cur):
                m = n - 1
                for u in range(2 * HG):
                    if cur:
                        q_unit(n, u)
                    if prev and u == 0:
                        turn_scores(m, 1, 0)
                        scores(m, 1, 1)
                        values_out(m, 3)
                    if prev and u == 1:
                        turn_scores(m, 1, 1)
                    if prev and u == 2:
                        turn_probs(m, 1, 0)
                    if prev and u == 3:
                        turn_probs(m, 1, 1)
                    if cur and u == 3:
                        scores(n, 0, 0)
                    if prev and u == 4:
                        pe.wait_ge(pt_lo, m * 4 + 4)
                        if cur:
                            for o in range(16):
                                output(m, o)
                    if not cur:
                        continue
                    if u == 4:
                        turn_scores(n, 0, 0)
                        scores(n, 0, 1)
                    if u == 5:
                        values_out(n, 0)
                        turn_scores(n, 0, 1)
                    if u == 6:
                        turn_probs(n, 0, 0)
                        values_out(n, 1)
                    if u == 7:
                        turn_probs(n, 0, 1)
                        values_out(n, 2)
                        scores(n, 1, 0)

            for s in range(STEPS_IN):
                if s < NKV:
                    kv_project(s)
                if s == 0:
                    pe.wait_ge(s_const, 16 * 8)
                if 0 <= s - 2 < TP:
                    turn_x(0, s - 2)
            pe.wait_ge(krot, NKV)
            pe.wait_ge(vst, NKV)
            for bp in range(BP):
                pe.wait_ge(xt_lo, (bp + 1) * TP)
                turns(pe, bp, turn)
                for s in range(STEPS_OUT):
                    if bp < BP - 1 and 0 <= s - X_LAG - 2 < TP:
                        turn_x(bp + 1, s - X_LAG - 2)
                    if s < TP:
                        for half in range(2):
                            output(bp * NKV + NKV - 1, 2 * s + half)
                    if 0 <= s - 2 < TP:
                        turn_x1(bp, s - 2)
                    if 0 <= s - 3 < TP:
                        logits(bp, s - 3)
                    if s - 4 in (RB, 2 * RB):
                        counts(bp * 2 + (s - 4) // RB - 1)
                pe.wait_ge(routed, (bp + 1) * TP // RB)

            pe.wait_ge(s_lists, 16)
            pe.wait_ge(e_chain, 1)
            for h in range(2):
                for c in range(2):
                    mm = pe.transpose(bank[4 + c][:, ts(h, P)], lists[:, h, c:2 * P:2], idn[:])
            mm.then_inc(lists_done, 1)
            pe.wait_ge(e_chain, E_CHAIN)

            def turn_rows(t):
                pe.wait_ge(s_gather, t * 16 + 16)
                wait(pe, xf_lo, t)
                for k in range(KC):
                    mm = pe.transpose(xf_ps[k // 4][:, ts(k % 4, P)], xg[:, ts(k, P)], idn[:])
                mm.then_inc(tt_done, 1)

            def finish(t, r):
                pe.wait_ge(h_done, t)
                pe.transpose(ht_ps[0:FI, 0:P], hm[:], idn[:]).then_inc(ht_done, 1)
                pe.wait_ge(ht_lo, t)
                for half in range(2):
                    cols = ts(half, HALF)
                    pe.matmul(y_ps[half][:], hth[:], dnh[:, r, cols], start=True, stop=False)
                    pe.matmul(y_ps[half][:], hth[:], dnl[:, r, cols], start=False, stop=False)
                    mm = pe.matmul(y_ps[half][:], htl[:], dnh[:, r, cols], start=False, stop=True)
                mm.then_inc(d_done, 1)

            def gate_up(t, r):
                pe.wait_ge(xf_lo, t + 1)
                for k in range(KC):
                    pe.matmul(gu_ps[:, 0:GW], xfh[:, k, :], guh[:, r, k, :], start=(k == 0), stop=False)
                    pe.matmul(gu_ps[:, 0:GW], xfh[:, k, :], gul[:, r, k, :], start=False, stop=False)
                    mm = pe.matmul(gu_ps[:, 0:GW], xfl[:, k, :], guh[:, r, k, :], start=False, stop=(k == KC - 1))
                mm.then_inc(gu_done, 1)

            def tile(t, r):
                turn_rows(t)
                finish(t, r)
                gate_up(t, r)

            def first(e, r, t, is_last):
                turn_rows(t)
                if not (isinstance(e, int) and e == 0):
                    finish(t, 1 - r)
                pe.wait_ge(w_lo, e + 1)
                gate_up(t, r)

            experts(pe, tile, first, lambda t: finish(t, (NE - 1) % 2))

        @block.vector
        def _(dve):
            dve.memset(ones[:], 1.0).then_inc(setup, 1)
            dve.memset(before[:, 0, :], 0.0).then_inc(setup, 1)
            dve.wait_ge(s_const, 16 * 8)

            def kv_rotate(g):
                r = g % 2
                dve.wait_ge(kproj, g + 1)
                wait(dve, s_kvout[r], g // 2 * 16)
                rows = slice(0, D // 2), slice(D // 2, D)
                kin = bank[4 + r][:, 0:B * SK].rearrange("p (b s) -> p b s", b=B)
                co = cos_sb[:, 0:SK].unsqueeze(1).broadcast_to([D, B, SK])
                si = sin_sb[:, 0:SK].unsqueeze(1).broadcast_to([D, B, SK])
                dve.tensor_tensor(k1[:, r, :].rearrange("p (b s) -> p b s", b=B), kin, co, ALU.mult)
                for lo in range(2):
                    ins = dve.tensor_tensor(k2[rows[lo], r, :].rearrange("p (b s) -> p b s", b=B), kin[rows[1 - lo]], si[rows[lo]], ALU.mult)
                ins.then_inc(krot, 1)
                dve.wait_ge(krot, g + 1)
                dve.tensor_tensor(k1[:, r, :], k1[:, r, :], k2[:, r, :], ALU.add).then_inc(kst, 1)

            def norm(w, bp, s):
                if 0 <= s < TP:
                    if w == 0:
                        dve.wait_ge(s_x[s], 16 * (bp + 1))
                    else:
                        dve.wait_ge(ov_free, 24 * (bp * NKV + NKV - 1) + 8 + 2 * s + 2)
                    for half in range(2):
                        ins = dve.bn_stats(stats[:, w, s % 2, half, :], acc[:, s, ts(half, HALF)])
                    ins.then_inc(stat_done[w], 1)
                if 0 <= s - 1 < TP:
                    t = s - 1
                    if w == 0:
                        wait(dve, xt_done[0], bp * TP + t - 1)
                        to = qr[:, 2 * (t % 2):2 * (t % 2) + 2, :].rearrange("p a q -> p (a q)")
                    else:
                        dve.wait_ge(s_x1[t], 16 * (bp + 1))
                        to = acc[:, t, :]
                    dve.wait_ge(rstd_done[w], bp * TP + t + 1)
                    dve.tensor_scalar(to, acc[:, t, :], mv[:, w, t % 2, 0:1], rstd[:, w, t % 2, :],
                                      ALU.subtract, ALU.mult).then_inc(xn_done[w], 1)
                if 0 <= s < TP:
                    dve.wait_ge(stat_done[w], bp * TP + s + 1)
                    dve.bn_aggr(mv[:, w, s % 2, :], stats[:, w, s % 2, :, :]).then_inc(aggr_done[w], 1)

            def x_low(bp, t):
                for kh in range(2):
                    dve.wait_ge(xt_hi, (bp * TP + t) * 2 + kh + 1)
                    ins = dve.tensor_tensor(xl[:, 4 * kh:4 * kh + 4, ts(t, P)], bank[2 + kh][:].rearrange("p (k t) -> p k t", k=4),
                                            xh[:, 4 * kh:4 * kh + 4, ts(t, P)], ALU.subtract)
                ins.then_inc(xt_lo, 1)

            for s in range(STEPS_IN):
                if 0 <= s - 3 < TP:
                    x_low(0, s - 3)
                if s < NKV:
                    kv_rotate(s)
                norm(0, 0, s)

            def rotate(n, u):
                j, b = u // 2, u % 2
                dve.wait_ge(q_done, n * 8 + u + 1)
                if j < 2:
                    wait(dve, s_done, n * 4 - 1 + b)
                else:
                    dve.wait_ge(s_done, n * 4 + b + 1)
                wait(dve, q_ready, n * 8 + u - 1)
                dve.tensor_tensor(qr[:, 2 * (j % 2) + b, :], q_ps[b][:], cos_sb[:], ALU.mult)
                dve.tensor_tensor(qt2[0:64, b, :], q_ps[b][64:128, :], sin_sb[0:64, :], ALU.mult)
                dve.tensor_tensor(qt2[64:128, b, :], q_ps[b][0:64, :], sin_sb[64:128, :], ALU.mult).then_inc(q_rot, 1)

            def mask_scores(m, c, b):
                s = m * 4 + (2 * c + b)
                dve.wait_ge(s_done, s + 1)
                wait(dve, t1_done, s)
                dve.tensor_tensor(soft[:, 0, 0:SK], st_ps[:, 0:SK], mask_sb[:], ALU.add).then_inc(st_mask, 1)

            def less_max(m, c, b):
                s = m * 4 + (2 * c + b)
                dve.wait_ge(t1_done, s + 1)
                sn = sn_ps[:].rearrange("p (g k) -> p g k", k=SK)
                dve.tensor_reduce(mx[:, b, :], sn, X, ALU.max).then_inc(mx_done, 1)
                dve.wait_ge(mx_done, s + 1)
                wait(dve, t2_done, s - 1)
                dve.tensor_tensor(soft[:, 1 + b, :].rearrange("p (g k) -> p g k", k=SK), sn,
                                  mx[:, b, :].unsqueeze(2).broadcast_to([P, 8, SK]), ALU.subtract).then_inc(sub_done, 1)

            def sums(m, c, b):
                s = m * 4 + (2 * c + b)
                dve.wait_ge(exp_done, s + 1)
                dve.tensor_reduce(sm[:, b, :], soft[:, 1 + b, :].rearrange("p (g k) -> p g k", k=SK), X, ALU.add).then_inc(sum_done, 1)
                dve.wait_ge(sum_done, s + 1)
                dve.reciprocal(rc[:, b, :], sm[:, b, :]).then_inc(rc_done, 1)

            def probs_low(m, c, b):
                s = m * 4 + (2 * c + b)
                dve.wait_ge(pt_hi, s + 1)
                dve.tensor_tensor(ptl[:, c, b, :], pt_ps[:], pth[:, c, b, :], ALU.subtract).then_inc(pt_lo, 1)

            def values_low(m, j):
                for half in range(2):
                    dve.wait_ge(vw_hi, m * 8 + 2 * j + half + 1)
                    ps = ov_ps[(2 * j + half) % 3]
                    for at in range(2):
                        rows, b = slice(64 * at, 64 * at + 64), at ^ (j % 2)
                        ins = dve.tensor_tensor(vwl[rows, j // 2, b, ts(half, HALF)], ps[rows, :], vwh[rows, j // 2, b, ts(half, HALF)], ALU.subtract)
                    ins.then_inc(ov_free, 1)

            def add_output(m, o):
                dve.wait_ge(ov_done, m * 24 + 8 + o + 1)
                part = acc[:, o // 2, ts(o % 2, HALF)]
                dve.tensor_tensor(part, part, ov_ps[(8 + o) % 3][:], ALU.add).then_inc(ov_free, 1)

            def turn(n, g, prev, cur):
                m = n - 1
                for u in range(2 * HG):
                    if cur:
                        rotate(n, u)
                    if prev and u == 0:
                        mask_scores(m, 1, 1)
                        less_max(m, 1, 0)
                        values_low(m, 3)
                        sums(m, 1, 0)
                    if prev and u == 1:
                        less_max(m, 1, 1)
                        sums(m, 1, 1)
                    if prev and u == 2:
                        probs_low(m, 1, 0)
                    if prev and u == 3:
                        probs_low(m, 1, 1)
                    if cur and u == 3:
                        mask_scores(n, 0, 0)
                    if prev and cur and u == 4:
                        for o in range(16):
                            add_output(m, o)
                    if not cur:
                        continue
                    if u == 4:
                        less_max(n, 0, 0)
                        mask_scores(n, 0, 1)
                        dve.wait_ge(v_hi, n + 1)
                        dve.tensor_tensor(vl[:], vraw[:], vh[:], ALU.subtract).then_inc(v_lo, 1)
                        sums(n, 0, 0)
                    if u == 5:
                        less_max(n, 0, 1)
                        values_low(n, 0)
                        sums(n, 0, 1)
                    if u == 6:
                        probs_low(n, 0, 0)
                        values_low(n, 1)
                    if u == 7:
                        probs_low(n, 0, 1)
                        values_low(n, 2)
                        mask_scores(n, 1, 0)


            chain = [0]

            def link(ins):
                chain[0] += 1
                ins.then_inc(r_chain, 1)
                dve.wait_ge(r_chain, chain[0])

            def route_top(q):
                h = q % (TP // RB)
                dve.wait_ge(lg_done, (q + 1) * RB)
                dve.tensor_copy(lg[:].rearrange("p t e -> p (t e)"), bank[4][:, h * RB * NE:(h + 1) * RB * NE]).then_inc(lg_taken, 1)
                dve.wait_ge(lg_taken, q + 1)
                for t in range(RB):
                    ins = dve.max(top[:, t, :], lg[:, t, :])
                link(ins)
                for t in range(RB):
                    ins = dve.max_index(top_i[:, t, :], top[:, t, :], lg[:, t, :])
                link(ins)
                link(dve.tensor_copy(top_f[:], top_i[:, :, 0:2].rearrange("p t k -> p k t")))
                dve.tensor_tensor(gap[:], top[:, :, 1], top[:, :, 0], ALU.subtract).then_inc(gap_done, 1)
                link(dve.tensor_tensor(hot[:, 0:2, :].rearrange("p k (t e) -> p (k t) e", e=NE), iota_e[:].unsqueeze(1).broadcast_to([P, 2 * RB, NE]),
                                       top_f[:].rearrange("p k t -> p (k t)").unsqueeze(2).broadcast_to([P, 2 * RB, NE]), ALU.is_equal))
                dve.tensor_tensor(hot[:, 2, :], hot[:, 0, :], hot[:, 1, :], ALU.add).then_inc(hot_done, 1)

            def route_slots(q):
                ps = ov_ps[q % (TP // RB)]
                dve.wait_ge(cnt_mm, q + 1)
                for t in range(RB):
                    i = q * RB + t
                    link(dve.tensor_tensor(before[:, i + 1, :], ps[:, (RB + t) * NE:(RB + t + 1) * NE], before[:, i, :], ALU.add))
                link(dve.tensor_tensor(pos[:], ps[:, 0:RB * NE],
                                       before[:, q * RB:(q + 1) * RB, :].rearrange("p t e -> p (t e)"), ALU.add))
                link(dve.tensor_tensor(pick[:], hot[:, 0:2, :], pos[:].unsqueeze(1).broadcast_to([P, 2, RB * NE]), ALU.mult))
                link(dve.tensor_reduce(pos_k[:].rearrange("p k t -> p (k t)"), pick[:].rearrange("p k (t e) -> p (k t) e", e=NE), X, ALU.add))
                link(dve.scalar_tensor_tensor(out=slot_f[:], in0=top_f[:], scalar=float(CAP), in1=pos_k[:], op0=ALU.mult, op1=ALU.add))
                dve.tensor_copy(slot_i[:, q, :, :], slot_f[:])
                dve.wait_ge(egap_done, q + 1)
                link(dve.tensor_scalar(den[:], egap[:], 1.0, None, ALU.add))
                link(dve.reciprocal(den[:], den[:]))
                link(dve.tensor_tensor(w1[:], den[:], tanh_f[:].broadcast_to([P, RB]), ALU.mult))
                dve.tensor_copy(entry[:, q, 0, :, 1], w1[:])
                dve.tensor_tensor(entry[:, q, 1, :, 1], w1[:], egap[:], ALU.mult)
                dve.tensor_copy(entry[:, q, 0, :, 0], token[:, q, :])
                dve.tensor_copy(entry[:, q, 1, :, 0], token[:, q, :]).then_inc(routed, 1)

            for bp in range(BP):
                turns(dve, bp, turn)
                for s in range(STEPS_OUT):
                    if s - 3 in (RB, 2 * RB):
                        route_top(bp * 2 + (s - 3) // RB - 1)
                    if bp < BP - 1 and 0 <= s - X_LAG - 3 < TP:
                        x_low(bp + 1, s - X_LAG - 3)
                    if s < TP:
                        for half in range(2):
                            add_output(bp * NKV + NKV - 1, 2 * s + half)
                    norm(1, bp, s)
                    if bp < BP - 1:
                        norm(0, bp + 1, s - X_LAG)
                    if s - 4 in (RB, 2 * RB):
                        route_slots(bp * 2 + (s - 4) // RB - 1)

            for t in range(TP):
                dve.wait_ge(s_xn[t], 16 * BP)
            at = [0]

            def link(ins):
                at[0] += 1
                ins.then_inc(e_chain, 1)
                dve.wait_ge(e_chain, at[0])

            link(dve.tensor_scalar(tile_n[:], before[:, B * QT, :], float(P - 1), None, ALU.add))
            link(dve.tensor_scalar(tile_n[:], tile_n[:], P.bit_length() - 1, None, ALU.arith_shift_right))
            link(dve.tensor_scalar(tile_n[:], tile_n[:], 1.0, None, ALU.max))
            link(dve.tensor_copy(pre[:, 0, :], tile_n[:]))
            for k in range(4):
                a, b, by = k % 2, 1 - k % 2, 2 ** k
                dve.tensor_copy(pre[:, b, 0:by], pre[:, a, 0:by])
                link(dve.tensor_tensor(pre[:, b, by:NE], pre[:, a, by:NE], pre[:, a, 0:NE - by], ALU.add))
            dve.memset(tile_at[:, 0:1], 0)
            link(dve.tensor_copy(tile_at[:, 1:NE + 1], pre[:, 0, :]))
            for w in (guh, gul):
                ins = dve.memset(w[:, :, :, 2 * FI:GW].bitcast(f32), 0.0)
            ins.then_inc(pads, 1)
            dve.wait_ge(lists_done, 1)
            dve.tensor_copy(row_all[:], bank[4][:, 0:2 * P]).then_inc(rows_done, 1)
            dve.tensor_copy(w_all[:], bank[5][:, 0:2 * P]).then_inc(rows_done, 1)
            dve.wait_ge(rows_done, 2)
            dve.tensor_copy(w_of[:, 0:ET], w_all[:, 0:ET]).then_inc(w_chain, 1)
            with dve.Fori(1, NE) as e:
                t0 = dve.value_load(tile_at[0:1, ds(e, 1)], min_val=1, max_val=MT)
                dve.wait_ge(w_chain, e)
                dve.tensor_copy(w_of[:, ds(t0, ET)], w_all[:, ds(e * ET, ET)]).then_inc(w_chain, 1)
            dve.wait_ge(w_chain, NE)

            def split_low(e, r):
                dve.wait_ge(w_hi, e + 1)
                dve.tensor_tensor(gul[:, r, :, 0:2 * FI], gu_raw[:, r, :].rearrange("p (k n) -> p k n", k=KC), guh[:, r, :, 0:2 * FI], ALU.subtract)
                dve.tensor_tensor(dnl[:, r, :], dn_raw[:, r, :], dnh[:, r, :], ALU.subtract).then_inc(w_lo, 1)

            def rows_low(t, half):
                dve.wait_ge(xf_hi, t * 2 + half + 1)
                rows = slice(4 * half, 4 * half + 4)
                return dve.tensor_tensor(xfl[:, rows, :], xf_ps[half][:].rearrange("p (k t) -> p k t", k=4), xfh[:, rows, :], ALU.subtract)

            def inner(t):
                dve.wait_ge(silu_done, t)
                dve.scalar_tensor_tensor(out=hm[:], in0=sg[:], scalar=w_of[:, ds(t - 1, 1)], in1=gu_ps[:, FI:2 * FI], op0=ALU.mult, op1=ALU.mult).then_inc(h_done, 1)

            def inner_low(t):
                dve.wait_ge(ht_hi, t)
                dve.tensor_tensor(htl[:], ht_ps[0:FI, 0:P], hth[:], ALU.subtract).then_inc(ht_lo, 1)

            def out_b(t):
                dve.wait_ge(d_done, t)
                dve.wait_ge(s_add, t * 16 + 16)
                dve.tensor_copy(ys[:, HALF:C], y_ps[1][:]).then_inc(y_b, 1)

            def tile(t, r):
                inner(t)
                rows_low(t, 0)
                inner_low(t)
                rows_low(t, 1).then_inc(xf_lo, 1)
                out_b(t)

            def first(e, r, t, is_last):
                if isinstance(e, int) and e == 0:
                    rows_low(t, 0)
                    rows_low(t, 1).then_inc(xf_lo, 1)
                else:
                    tile(t, r)
                if not is_last:
                    split_low(e + 1, 1 - r)

            def tail(t):
                inner(t)
                inner_low(t)
                out_b(t)

            split_low(0, 0)
            experts(dve, tile, first, tail)

        @block.scalar
        def _(act):
            act.wait_ge(s_const, 16 * 8)
            act.activation(tanh_x[:], gates_raw[:, 0:1], ACT.Tanh).then_inc(tanh_done, 1)
            act.activation(tanh_f[:], gates_raw[:, 1:2], ACT.Tanh).then_inc(tanh_done, 1)
            act.wait_ge(tanh_done, 2)

            def kv_scale(g):
                r = g % 2
                act.wait_ge(vproj, g + 1)
                wait(act, s_kvout[2 + r], g // 2 * 16)
                act.activation(v1[:, r, :], bank[6 + r][:, 0:B * SK], ACT.Copy, scale=tanh_x[:, 0:1]).then_inc(vst, 1)

            def split_wq(n, u):
                h = n * 8 + u
                act.wait_ge(s_wq[u % 2], n * 64 + (u // 2) * 16 + 16)
                wait(act, q_done, n * 8 + u - u % 2 - 2)
                act.activation(wqh[:, u % 4, :], wq_raw[:, u % 2, :], ACT.Copy).then_inc(wq_hi, 1)

            def split_wd(n, u):
                act.wait_ge(s_wd[u % 2], n * 64 + (u // 2) * 16 + 16)
                wait(act, ov_done, n * 24 + u - 1 if u >= 2 else n * 24 - 17 + u)
                act.activation(wdh[:, u % 2, :], wd_raw[:, u % 2, :], ACT.Copy).then_inc(wd_hi, 1)

            def x_high(bp, t):
                act.wait_ge(xt_done[0], bp * TP + t + 1)
                for kh in range(2):
                    act.activation(xh[:, 4 * kh:4 * kh + 4, ts(t, P)],
                                   bank[2 + kh][:].rearrange("p (k t) -> p k t", k=4), ACT.Copy).then_inc(xt_hi, 1)

            def copy_scores(m, c, b):
                s = m * 4 + (2 * c + b)
                act.wait_ge(st_mask, s + 1)
                act.activation(soft[:, 0, SK:S], st_ps[:, SK:S], ACT.Copy).then_inc(st_copy, 1)

            def exps(m, c, b):
                s = m * 4 + (2 * c + b)
                act.wait_ge(sub_done, s + 1)
                act.activation(soft[:, 1 + b, :], soft[:, 1 + b, :], ACT.Exp, scale=SCALE).then_inc(exp_done, 1)

            def probs_high(m, c, b):
                s = m * 4 + (2 * c + b)
                act.wait_ge(t2_done, s + 1)
                wait(act, ov_done, m * 24)
                act.activation(pth[:, c, b, :], pt_ps[:], ACT.Copy).then_inc(pt_hi, 1)

            def values_high(m, j):
                for half in range(2):
                    act.wait_ge(ov_done, m * 24 + 2 * j + half + 1)
                    ps = ov_ps[(2 * j + half) % 3]
                    for at in range(2):
                        rows, b = slice(64 * at, 64 * at + 64), at ^ (j % 2)
                        ins = act.activation(vwh[rows, j // 2, b, ts(half, HALF)], ps[rows, :], ACT.Copy)
                    ins.then_inc(vw_hi, 1)

            def turn(n, g, prev, cur):
                m = n - 1
                last = isinstance(n, int) and n == NG - 1
                for u in range(2 * HG):
                    if cur and u < 6:
                        split_wq(n, u + 2)
                    elif cur and not last:
                        split_wq(n + 1, u - 6)
                    if prev and u == 0:
                        split_wd(m, 6)
                        split_wd(m, 7)
                        copy_scores(m, 1, 1)
                        values_high(m, 3)
                        exps(m, 1, 0)
                    if prev and u == 1:
                        exps(m, 1, 1)
                    if prev and u == 2:
                        probs_high(m, 1, 0)
                    if prev and u == 3:
                        probs_high(m, 1, 1)
                    if not cur:
                        continue
                    if u == 3:
                        split_wd(n, 0)
                        copy_scores(n, 0, 0)
                    if u == 4:
                        split_wd(n, 1)
                        act.wait_ge(s_v, n * 32 + 32)
                        wait(act, ov_done, n * 24 - 16)
                        act.activation(vh[:], vraw[:], ACT.Copy).then_inc(v_hi, 1)
                        copy_scores(n, 0, 1)
                        exps(n, 0, 0)
                    if u == 5:
                        values_high(n, 0)
                        exps(n, 0, 1)
                    if u == 6:
                        split_wd(n, 2)
                        split_wd(n, 3)
                        probs_high(n, 0, 0)
                        values_high(n, 1)
                    if u == 7:
                        split_wd(n, 4)
                        split_wd(n, 5)
                        probs_high(n, 0, 1)
                        values_high(n, 2)
                        copy_scores(n, 1, 0)

            def copy_tile(bp, t):
                i = bp * TP + t
                act.wait_ge(xt_done[1], i + 1)
                wait(act, lg_done, i - 1)
                for kh in range(2):
                    ins = act.activation(xt2[t % 2][:, 4 * kh:4 * kh + 4, :], bank[kh][:].rearrange("p (k t) -> p k t", k=4), ACT.Copy)
                ins.then_inc(xt2_done, 1)

            for s in range(STEPS_IN):
                if s < NKV:
                    kv_scale(s)
                if 0 <= s - 2 < TP:
                    x_high(0, s - 2)
            for u in range(2):
                split_wq(0, u)
            act.wait_ge(s_slot0, 16 * (NE * ET // P))
            for bp in range(BP):
                turns(act, bp, turn, last_apart=True)
                if bp < BP - 1:
                    act.wait_ge(q_done, 8 * NKV * (bp + 1))
                for s in range(STEPS_OUT):
                    if bp < BP - 1 and 0 <= s - X_LAG - 2 < TP:
                        x_high(bp + 1, s - X_LAG - 2)
                    if 0 <= s - 2 < TP:
                        copy_tile(bp, s - 2)
                    if s - 3 in (RB, 2 * RB):
                        q = bp * 2 + (s - 3) // RB - 1
                        act.wait_ge(gap_done, q + 1)
                        act.activation(egap[:], gap[:], ACT.Exp).then_inc(egap_done, 1)

            def split_high(e, r):
                act.wait_ge(s_gu[r], e // 2 * 16 + 16 if isinstance(e, int) else (e - r) * 8 + 16)
                act.activation(guh[:, r, :, 0:2 * FI], gu_raw[:, r, :].rearrange("p (k n) -> p k n", k=KC), ACT.Copy)
                act.wait_ge(s_dn[r], e // 2 * 16 + 16 if isinstance(e, int) else (e - r) * 8 + 16)
                act.activation(dnh[:, r, :], dn_raw[:, r, :], ACT.Copy).then_inc(w_hi, 1)

            def silu(t):
                act.wait_ge(gu_done, t)
                act.activation(sg[:], gu_ps[:, 0:FI], ACT.Silu).then_inc(silu_done, 1)

            def rows_high(t):
                act.wait_ge(tt_done, t + 1)
                for half in range(2):
                    act.activation(xfh[:, 4 * half:4 * half + 4, :], xf_ps[half][:].rearrange("p (k t) -> p k t", k=4), ACT.Copy).then_inc(xf_hi, 1)

            def inner_high(t):
                act.wait_ge(ht_done, t)
                act.activation(hth[:], ht_ps[0:FI, 0:P], ACT.Copy).then_inc(ht_hi, 1)

            def out_a(t):
                act.wait_ge(d_done, t)
                act.wait_ge(s_add, t * 16 + 16)
                act.activation(ys[:, 0:HALF], y_ps[0][:], ACT.Copy).then_inc(y_a, 1)

            def tile(t, r):
                silu(t)
                rows_high(t)
                inner_high(t)
                out_a(t)

            def first(e, r, t, is_last):
                if isinstance(e, int) and e == 0:
                    rows_high(t)
                else:
                    tile(t, r)
                if not is_last:
                    split_high(e + 1, 1 - r)

            def tail(t):
                silu(t)
                inner_high(t)
                out_a(t)

            act.wait_ge(pads, 1)
            split_high(0, 0)
            act.wait_ge(e_chain, E_CHAIN)
            experts(act, tile, first, tail)

        @block.gpsimd
        def _(pool):
            pool.memset(eps_half[:], -0.5).then_inc(iotas, 1)
            pool.iota(iota_e[:], [[1, NE]], base=0, channel_multiplier=0, allow_small_or_imprecise_dtypes=True).then_inc(iotas, 1)
            pool.iota(token[:].rearrange("p q t -> p (q t)"), [[P, B * QT]], base=0, channel_multiplier=1, allow_small_or_imprecise_dtypes=True).then_inc(iotas, 1)
            pool.iota(empty[:, :, 0], [[1, P]], base=T, channel_multiplier=0, allow_small_or_imprecise_dtypes=True).then_inc(iotas, 1)
            pool.memset(empty[:, :, 1], 0.0).then_inc(iotas, 1)
            pool.wait_ge(iotas, 5)
            for h in range(NE * ET // P):
                pool.dma_start(slots_hbm.rearrange("(a s) c -> a (s c)", s=P)[h * P:(h + 1) * P, :],
                               empty[:].rearrange("p s c -> p (s c)")).then_inc(s_slot0, 16)

            def split_wq(n, u):
                pool.wait_ge(wq_hi, n * 8 + u + 1)
                pool.tensor_tensor(wql[:, u % 4, :], wq_raw[:, u % 2, :], wqh[:, u % 4, :], ALU.subtract).then_inc(wq_lo, 1)

            def split_wd(n, u):
                pool.wait_ge(wd_hi, n * 8 + u + 1)
                pool.tensor_tensor(wdl[:, u % 2, :], wd_raw[:, u % 2, :], wdh[:, u % 2, :], ALU.subtract).then_inc(wd_lo, 1)

            def norm(w, bp, t):
                r = t % 2
                pool.wait_ge(aggr_done[w], bp * TP + t + 1)
                pool.tensor_scalar(var_eps[:, w, r, :], mv[:, w, r, 1:2], EPS, None, ALU.add).then_inc(var_done[w], 1)
                pool.wait_ge(var_done[w], bp * TP + t + 1)
                pool.tensor_tensor(rstd[:, w, r, :], var_eps[:, w, r, :], eps_half[:], ALU.pow).then_inc(rstd_done[w], 1)

            def scatter_slots(i):
                q, t = i // RB, i % RB
                pool.wait_ge(routed, q + 1)
                if i == 0:
                    pool.wait_ge(s_slot0, 16 * (NE * ET // P))
                for k in range(2):
                    pool.indirect_dma_start(out=slots_hbm, out_offset=bass.IndirectOffsetOnAxis(ap=slot_i[:, q, k, t:t + 1], axis=0),
                                            in_=entry[:, q, k, t, :], in_offset=None).then_inc(s_scat[k], 16)

            def add_halves(n, u):
                slot = 2 * (u // 2 % 2) + u % 2
                pool.wait_ge(q_rot, n * 8 + u + 1)
                pool.tensor_tensor(qr[:, slot, :], qr[:, slot, :], qt2[:, u % 2, :], ALU.add).then_inc(q_ready, 1)

            def probs(m, c, b):
                s = m * 4 + (2 * c + b)
                pool.wait_ge(rc_done, s + 1)
                part = soft[:, 1 + b, :].rearrange("p (g k) -> p g k", k=SK)
                pool.tensor_tensor(part, part, rc[:, b, :].unsqueeze(2).broadcast_to([P, 8, SK]), ALU.mult).then_inc(p_done, 1)

            def turn(n, g, prev, cur):
                m = n - 1
                last = isinstance(n, int) and n == NG - 1
                for u in range(2 * HG):
                    if cur and u < 6:
                        split_wq(n, u + 2)
                    elif cur and not last:
                        split_wq(n + 1, u - 6)
                    if prev and u == 0:
                        split_wd(m, 6)
                        split_wd(m, 7)
                    if prev and u == 1:
                        probs(m, 1, 0)
                    if prev and u == 2:
                        probs(m, 1, 1)
                    if not cur:
                        continue
                    for d in {3: (0,), 4: (1,), 6: (2, 3), 7: (4, 5)}.get(u, ()):
                        split_wd(n, d)
                    if u == 5:
                        probs(n, 0, 0)
                    if u == 6:
                        probs(n, 0, 1)
                    add_halves(n, u)

            for t in range(TP):
                norm(0, 0, t)
            for u in range(2):
                split_wq(0, u)
            for bp in range(BP):
                turns(pool, bp, turn, last_apart=True)
                for s in range(STEPS_OUT):
                    if s < TP:
                        norm(1, bp, s)
                    if bp < BP - 1 and 0 <= s - X_LAG < TP:
                        norm(0, bp + 1, s - X_LAG)
                    if bp == BP - 1 and s < TP:
                        scatter_slots(s)
            for i in range(TP, 2 * TP):
                scatter_slots(i)

            for t in range(TP):
                pool.wait_ge(s_xn[t], 16 * BP)
            pool.memset(row_s[:], 0).then_inc(s_set, 1)
            pool.memset(ys[:, 0:HALF], 0.0).then_inc(y_a, 1)
            pool.memset(ys[:, HALF:C], 0.0).then_inc(y_b, 1)
            pool.wait_ge(y_a, 1)
            pool.wait_ge(y_b, 1)
            pool.dma_start(xn_hbm[T:T + P, :], ys[:]).then_inc(s_add, 16)
            pool.wait_ge(s_add, 16)
            pool.dma_start(out[T:T + P, :], ys[:]).then_inc(s_add, 16)
            pool.wait_ge(rows_done, 2)
            pool.wait_ge(e_chain, E_CHAIN)
            pool.tensor_copy(row_of[:, 0:ET], row_all[:, 0:ET]).then_inc(rows_chain, 1)
            with pool.Fori(1, NE) as e:
                t0 = pool.value_load(tile_at[0:1, ds(e, 1)], min_val=1, max_val=MT)
                pool.wait_ge(rows_chain, e)
                pool.tensor_copy(row_of[:, ds(t0, ET)], row_all[:, ds(e * ET, ET)]).then_inc(rows_chain, 1)
            pool.wait_ge(rows_chain, NE)
            total = pool.value_load(tile_at[0:1, NE:NE + 1], min_val=NE, max_val=MT)

            def gather(t):
                if not (isinstance(t, int) and t == 0):
                    pool.wait_ge(s_gather, t * 16)
                    pool.wait_ge(tt_done, t)
                pool.tensor_copy(row_g[:], row_of[:, ds(t, 1)]).then_inc(g_set, 1)
                pool.wait_ge(g_set, t + 1)
                pool.sem_inc(g_seen, 1)
                pool.indirect_dma_start(out=xg[:], out_offset=None, in_=xn_hbm,
                                        in_offset=bass.IndirectOffsetOnAxis(ap=row_g[:, 0:1], axis=0)).then_inc(s_gather, 16)

            def scatter(t):
                pool.wait_ge(y_a, t)
                pool.wait_ge(y_b, t)
                pool.wait_ge(s_add, t * 16)
                pool.tensor_copy(row_s[:], row_of[:, ds(t - 2, 1)]).then_inc(s_set, 1)
                pool.wait_ge(s_set, t)
                pool.sem_inc(s_seen, 1)
                pool.indirect_dma_start(out=out, out_offset=bass.IndirectOffsetOnAxis(ap=row_s[:, 0:1], axis=0),
                                        in_=ys[:], in_offset=None, compute_op=ALU.add).then_inc(s_add, 16)

            gather(0)
            gather(1)
            with pool.Fori(2, total) as t:
                gather(t)
                scatter(t)
            scatter(total)
            scatter(total + 1)
            pool.wait_ge(s_add, total * 16 + 32)


def _tables():
    inv = (1.0 / (np.float32(10000.0) ** (np.arange(0, D, 2, dtype=np.float32) / np.float32(D)))).astype(np.float32)
    ang = (np.arange(S, dtype=np.float32)[:, None] * inv[None, :]).astype(np.float32)
    c, s = np.cos(ang).astype(np.float32).T, np.sin(ang).astype(np.float32).T
    key, query = np.arange(P)[:, None] % SK, np.arange(SK)[None, :]
    return {
        "cos": np.ascontiguousarray(np.concatenate([c, c], 0)),
        "sin": np.ascontiguousarray(np.concatenate([-s, s], 0)),
        "mask": np.where(key <= query, 0.0, MASKED).astype(np.float32),
        "ident": np.eye(P, dtype=np.float32),
        "tri": np.triu(np.ones((P, P), np.float32), 1),
    }


def kernel(x, ctx_4096, g_xattn, g_ffn, L0_xattn_Wq, L0_xattn_Wk, L0_xattn_Wv, L0_xattn_Wd, L0_ffn_gate_w, L0_ffn_u, L0_ffn_g, L0_ffn_d):
    import concourse.bacc as bacc
    from concourse.bass_utils import run_bass_kernel_spmd

    def lay(a, *order_shape):
        return np.ascontiguousarray(a)

    x, ctx = np.asarray(x), np.asarray(ctx_4096)
    wq, wk, wv, wd = (np.asarray(a) for a in (L0_xattn_Wq, L0_xattn_Wk, L0_xattn_Wv, L0_xattn_Wd))
    gate, u, g, d = (np.asarray(a) for a in (L0_ffn_gate_w, L0_ffn_u, L0_ffn_g, L0_ffn_d))

    def by_head(w, heads):
        return lay(w.reshape(heads, D, KC, P).transpose(0, 3, 2, 1).reshape(heads, P, KC * D))

    arrays = {
        "x": lay(x.reshape(T, C)),
        "ctx_t": lay(ctx.reshape(B * SK, KC, P).transpose(2, 1, 0)),
        "g_x": lay(np.asarray(g_xattn).reshape(1)),
        "g_f": lay(np.asarray(g_ffn).reshape(1)),
        "wq": by_head(wq, NH),
        "wk": by_head(wk, NKV),
        "wv": by_head(wv, NKV),
        "wd": lay(wd.reshape(C, NH, D).transpose(1, 2, 0)),
        "gate": lay(gate.reshape(NE, KC, P).transpose(2, 1, 0)),
        "gu": lay(np.stack([g.reshape(NE, FI, KC, P), u.reshape(NE, FI, KC, P)], 1).transpose(0, 4, 3, 1, 2).reshape(NE, P, KC, 2 * FI)),
        "dn": lay(d.reshape(C, NE, FI).transpose(1, 2, 0)),
        **_tables(),
    }
    nc = bacc.Bacc("TRN2", target_bir_lowering=False, num_devices=1)
    args = {n: nc.dram_tensor(f"{n}_dram", a.shape, mybir.dt.from_np(a.dtype), kind="ExternalInput").ap() for n, a in arrays.items()}
    out = nc.dram_tensor("out_dram", (T + P, C), mybir.dt.float32, kind="ExternalOutput").ap()
    program(nc, out=out, **args)
    r = run_bass_kernel_spmd(nc, [{f"{n}_dram": a for n, a in arrays.items()}], core_ids=[0])
    return r.results[0]["out_dram"][:T].reshape(B, S, C)
```
